# Optimizing a Trainium2 kernel written in Bass

```python
import numpy as np
import jax
import jax.numpy as jnp

def _softmax(x, axis=-1):
    return jax.nn.softmax(x, axis=axis)

def _gelu(x):
    return jax.nn.gelu(x, approximate=True)

def _silu(x):
    return jax.nn.silu(x)

def _sigmoid(x):
    return jax.nn.sigmoid(x)

def _layernorm(x, axis=-1, eps=1e-05):
    m = jnp.mean(x, axis=axis, keepdims=True)
    v = jnp.var(x, axis=axis, keepdims=True)
    return (x - m) / jnp.sqrt(v + eps)

def _scatter_add(tgt, idx, src, axis=0):
    return tgt.at[idx].add(src)

def _segment_sum(src, seg, n):
    return jax.ops.segment_sum(src, seg, n)
kernel_name = 'mk_decoder_postln_d1_seqx_r2_c605c0'

def setup_inputs(seed: int=0):
    np.random.seed(seed)
    _w = jnp.asarray

    def _rec_inputs():
        import jax
        import jax.numpy as jnp
        _rk = jax.random.key(seed)
        x = 4.136e-05 + 0.9999 * jax.random.normal(jax.random.fold_in(_rk, 1), (8, 512, 512), jnp.float32)
        _lenS = 512 - jax.random.randint(jax.random.fold_in(_rk, 7), (8,), 0, max(1, 512 // 4) + 1, jnp.int32)
        _lenS2 = 120 - jax.random.randint(jax.random.fold_in(_rk, 8), (8,), 0, max(1, 120 // 4) + 1, jnp.int32)
        _ctx_1024P = jax.random.normal(jax.random.fold_in(_rk, 11), (8, 16, 512), jnp.float32)
        _ctx_1024c = jax.random.dirichlet(jax.random.fold_in(_rk, 511), 0.3 * jnp.ones((16,), jnp.float32), (8, 120))
        _ctx_1024t = jnp.einsum('bsk,bkd->bsd', _ctx_1024c, _ctx_1024P)
        _ctx_1024t = _ctx_1024t * jax.lax.rsqrt(jnp.mean(jnp.square(_ctx_1024t)) + 1e-12) * 0.953939
        ctx_1024 = 7.22013e-05 + 1.00017 * (_ctx_1024t + 0.3 * jax.random.normal(jax.random.fold_in(_rk, 611), (8, 120, 512), jnp.float32))
        return (x, ctx_1024)
    x, ctx_1024 = _rec_inputs()

    def _L0_attn_setup():
        import jax, jax.numpy as jnp
        import numpy as np
        B, N, D = (4, 1024, 512)
        H = 16
        HD = D // H
        SCALE = 1.0 / HD
        NEG = -10000.0
        THETA = 10000.0

        def _rope(t):
            d, n = (t.shape[-1], t.shape[-2])
            inv_freq = 1.0 / THETA ** (jnp.arange(0, d, 2, dtype=jnp.float32) / d)
            ang = jnp.arange(n, dtype=jnp.float32)[:, None] * inv_freq[None, :]
            cos = jnp.repeat(jnp.cos(ang), 2, axis=-1)
            sin = jnp.repeat(jnp.sin(ang), 2, axis=-1)
            x1, x2 = (t[..., ::2], t[..., 1::2])
            rot = jnp.stack([-x2, x1], axis=-1).reshape(t.shape)
            return t * cos + rot * sin
        key = jax.random.key(seed)
        ks = jax.random.split(key, 6)
        s = (1.0 / D) ** 0.5
        return {'x': jax.random.normal(ks[0], (B, N, D), jnp.float32), 'Wq': jax.random.normal(ks[1], (D, D), jnp.float32) * s, 'Wk': jax.random.normal(ks[2], (D, D), jnp.float32) * s, 'Wv': jax.random.normal(ks[3], (D, D), jnp.float32) * s, 'Wo': jax.random.normal(ks[4], (D, D), jnp.float32) * s, 'bo': jnp.zeros((D,), jnp.float32)}
    _L0_attn_all = _L0_attn_setup()
    _L0_attn_in = {k: v for k, v in _L0_attn_all.items() if k in ('Wq', 'Wk', 'Wv', 'Wo', 'bo')}
    del _L0_attn_all

    def _L0_xattn_setup():
        import jax, jax.numpy as jnp
        import numpy as np
        B, L_Q, L_KV, D, H = (4, 1024, 1024, 512, 16)
        key = jax.random.key(seed)
        ks = jax.random.split(key, 11)
        s = 0.02
        return {'kv': jax.random.normal(ks[0], (B, L_KV, D), dtype=jnp.float32), 'q': jax.random.normal(ks[1], (B, L_Q, D), dtype=jnp.float32), 'Wq': jax.random.normal(ks[2], (D, D), dtype=jnp.float32) * s, 'bq': jnp.zeros((D,), dtype=jnp.float32), 'Wk': jax.random.normal(ks[3], (D, D), dtype=jnp.float32) * s, 'bk': jnp.zeros((D,), dtype=jnp.float32), 'Wv': jax.random.normal(ks[4], (D, D), dtype=jnp.float32) * s, 'bv': jnp.zeros((D,), dtype=jnp.float32), 'Wo': jax.random.normal(ks[5], (D, D), dtype=jnp.float32) * s, 'bo': jnp.zeros((D,), dtype=jnp.float32)}
    _L0_xattn_all = _L0_xattn_setup()
    _L0_xattn_in = {k: v for k, v in _L0_xattn_all.items() if k in ('Wq', 'bq', 'Wk', 'bk', 'Wv', 'bv', 'Wo', 'bo')}
    del _L0_xattn_all

    def _L0_ffn_setup():
        import jax, jax.numpy as jnp
        import numpy as np
        HID = 512
        INTER = 2048
        RDIM = 128
        HEADS = 4
        NUM_EXPERTS = 8192
        NUM_KEYS = 128
        TOPK = 8
        B, T = (2, 1024)
        key = jax.random.key(seed)
        ks = jax.random.split(key, 8)
        s = lambda fan_in: 1.0 / np.sqrt(fan_in)
        return {'hidden_states': jax.random.normal(ks[0], (B, T, HID), jnp.float32), 'Wq': jax.random.normal(ks[1], (HEADS * RDIM, HID), jnp.float32) * s(HID), 'keys': jax.random.normal(ks[2], (HEADS, NUM_KEYS, 2, RDIM // 2), jnp.float32) * s(RDIM // 2), 'down_embed': jax.random.normal(ks[3], (NUM_EXPERTS, HID), jnp.float32) * 0.02, 'up_embed': jax.random.normal(ks[4], (NUM_EXPERTS, HID), jnp.float32) * 0.02, 'Wg': jax.random.normal(ks[5], (INTER, HID), jnp.float32) * s(HID), 'Wu': jax.random.normal(ks[6], (INTER, HID), jnp.float32) * s(HID), 'Wd': jax.random.normal(ks[7], (HID, INTER), jnp.float32) * s(INTER)}
    _L0_ffn_all = _L0_ffn_setup()
    _L0_ffn_in = {k: v for k, v in _L0_ffn_all.items() if k in ('Wq', 'keys', 'down_embed', 'up_embed', 'Wg', 'Wu', 'Wd')}
    del _L0_ffn_all
    return {'x': x, 'ctx_1024': ctx_1024, 'L0_attn_Wq': _L0_attn_in['Wq'], 'L0_attn_Wk': _L0_attn_in['Wk'], 'L0_attn_Wv': _L0_attn_in['Wv'], 'L0_attn_Wo': _L0_attn_in['Wo'], 'L0_attn_bo': _L0_attn_in['bo'], 'L0_xattn_Wq': _L0_xattn_in['Wq'], 'L0_xattn_bq': _L0_xattn_in['bq'], 'L0_xattn_Wk': _L0_xattn_in['Wk'], 'L0_xattn_bk': _L0_xattn_in['bk'], 'L0_xattn_Wv': _L0_xattn_in['Wv'], 'L0_xattn_bv': _L0_xattn_in['bv'], 'L0_xattn_Wo': _L0_xattn_in['Wo'], 'L0_xattn_bo': _L0_xattn_in['bo'], 'L0_ffn_Wq': _L0_ffn_in['Wq'], 'L0_ffn_keys': _L0_ffn_in['keys'], 'L0_ffn_down_embed': _L0_ffn_in['down_embed'], 'L0_ffn_up_embed': _L0_ffn_in['up_embed'], 'L0_ffn_Wg': _L0_ffn_in['Wg'], 'L0_ffn_Wu': _L0_ffn_in['Wu'], 'L0_ffn_Wd': _L0_ffn_in['Wd']}

def reference(x, ctx_1024, L0_attn_Wq, L0_attn_Wk, L0_attn_Wv, L0_attn_Wo, L0_attn_bo, L0_xattn_Wq, L0_xattn_bq, L0_xattn_Wk, L0_xattn_bk, L0_xattn_Wv, L0_xattn_bv, L0_xattn_Wo, L0_xattn_bo, L0_ffn_Wq, L0_ffn_keys, L0_ffn_down_embed, L0_ffn_up_embed, L0_ffn_Wg, L0_ffn_Wu, L0_ffn_Wd):
    import jax
    import jax.numpy as jnp

    def _L0_attn_ref(x, Wq, Wk, Wv, Wo, bo):
        import jax, jax.numpy as jnp
        import numpy as np
        B, N, D = (4, 1024, 512)
        H = 16
        HD = D // H
        SCALE = 1.0 / HD
        NEG = -10000.0
        THETA = 10000.0

        def _rope(t):
            d, n = (t.shape[-1], t.shape[-2])
            inv_freq = 1.0 / THETA ** (jnp.arange(0, d, 2, dtype=jnp.float32) / d)
            ang = jnp.arange(n, dtype=jnp.float32)[:, None] * inv_freq[None, :]
            cos = jnp.repeat(jnp.cos(ang), 2, axis=-1)
            sin = jnp.repeat(jnp.sin(ang), 2, axis=-1)
            x1, x2 = (t[..., ::2], t[..., 1::2])
            rot = jnp.stack([-x2, x1], axis=-1).reshape(t.shape)
            return t * cos + rot * sin
        b, n, _ = x.shape
        q = (x @ Wq.T).reshape(b, n, H, HD).transpose(0, 2, 1, 3)
        k = (x @ Wk.T).reshape(b, n, H, HD).transpose(0, 2, 1, 3)
        v = (x @ Wv.T).reshape(b, n, H, HD).transpose(0, 2, 1, 3)
        q = _rope(q)
        k = _rope(k)
        i = jnp.arange(n)
        add_mask = jnp.where(i[:, None] >= i[None, :], 0.0, NEG).astype(x.dtype)
        scores = jnp.einsum('bhqd,bhkd->bhqk', q, k) * SCALE + add_mask
        attn = jax.nn.softmax(scores, axis=-1)
        out = jnp.einsum('bhqk,bhkd->bhqd', attn, v)
        out = out.transpose(0, 2, 1, 3).reshape(b, n, H * HD)
        return out @ Wo.T + bo

    def _L0_xattn_ref(kv, q, Wq, bq, Wk, bk, Wv, bv, Wo, bo):
        import jax, jax.numpy as jnp
        import numpy as np
        B, L_Q, L_KV, D, H = (4, 1024, 1024, 512, 16)
        Bb, Lkv, Dm = kv.shape
        Lq = q.shape[1]
        hd = Dm // H
        scale = hd ** (-0.5)
        qh = (q @ Wq.T + bq).reshape(Bb, Lq, H, hd).transpose(0, 2, 1, 3)
        kh = (kv @ Wk.T + bk).reshape(Bb, Lkv, H, hd).transpose(0, 2, 1, 3)
        vh = (kv @ Wv.T + bv).reshape(Bb, Lkv, H, hd).transpose(0, 2, 1, 3)
        scores = jnp.einsum('bhqd,bhkd->bhqk', qh, kh) * scale
        mask = jnp.arange(Lkv)[None, :] <= jnp.arange(Lq)[:, None]
        scores = jnp.where(mask[None, None], scores, -jnp.inf)
        attn = jax.nn.softmax(scores, axis=-1)
        out = jnp.einsum('bhqk,bhkd->bhqd', attn, vh)
        out = out.transpose(0, 2, 1, 3).reshape(Bb, Lq, Dm)
        return out @ Wo.T + bo

    def _L0_ffn_ref(hidden_states, Wq, keys, down_embed, up_embed, Wg, Wu, Wd):
        import jax, jax.numpy as jnp
        import numpy as np
        HID = 512
        INTER = 2048
        RDIM = 128
        HEADS = 4
        NUM_EXPERTS = 8192
        NUM_KEYS = 128
        TOPK = 8
        B, T = (2, 1024)
        b, t, _ = hidden_states.shape
        q = hidden_states @ Wq.T
        q = q.reshape(b, t, 2, HEADS, RDIM // 2)
        q = jnp.transpose(q, (2, 0, 1, 3, 4))
        sim = jnp.einsum('pbthn,hkpn->pbthk', q, keys)
        sx, ix = jax.lax.top_k(sim[0], TOPK)
        sy, iy = jax.lax.top_k(sim[1], TOPK)
        all_scores = (sx[..., :, None] + sy[..., None, :]).reshape(b, t, HEADS, TOPK * TOPK)
        all_indices = (ix[..., :, None] * NUM_KEYS + iy[..., None, :]).reshape(b, t, HEADS, TOPK * TOPK)
        scores, pk = jax.lax.top_k(all_scores, TOPK)
        indices = jnp.take_along_axis(all_indices, pk, axis=-1)
        down = down_embed[indices]
        up = up_embed[indices]
        w = jnp.einsum('btd,bthkd->bthk', hidden_states, down)
        w = jax.nn.silu(w) * jax.nn.softmax(scores, axis=-1)
        experts_states = jnp.einsum('bthk,bthkd->btd', w, up)
        mlp = jax.nn.silu(hidden_states @ Wg.T) * (hidden_states @ Wu.T) @ Wd.T
        return mlp + experts_states
    x = _layernorm(x + _L0_attn_ref(x, L0_attn_Wq, L0_attn_Wk, L0_attn_Wv, L0_attn_Wo, L0_attn_bo), axis=-1)
    x = _layernorm(x + _L0_xattn_ref(ctx_1024, x, L0_xattn_Wq, L0_xattn_bq, L0_xattn_Wk, L0_xattn_bk, L0_xattn_Wv, L0_xattn_bv, L0_xattn_Wo, L0_xattn_bo), axis=-1)
    x = _layernorm(x + _L0_ffn_ref(x, L0_ffn_Wq, L0_ffn_keys, L0_ffn_down_embed, L0_ffn_up_embed, L0_ffn_Wg, L0_ffn_Wu, L0_ffn_Wd), axis=-1)
    return x

_drawn_inputs = setup_inputs


def setup_inputs(seed=0):
    import zlib

    import numpy as np

    out = dict(_drawn_inputs(seed))
    spreads = {'L0_attn_bo': (0.0, 0.1),
     'L0_xattn_bq': (0.0, 0.8),
     'L0_xattn_bk': (0.0, 0.8),
     'L0_xattn_bv': (0.0, 0.1),
     'L0_xattn_bo': (0.0, 0.1)}
    factors = {'L0_attn_Wq': 2.709,
     'L0_xattn_Wq': 6.244,
     'L0_xattn_Wk': 6.147,
     'L0_ffn_Wq': 8.0,
     'L0_ffn_keys': 8.0,
     'L0_ffn_down_embed': 6.229,
     'L0_ffn_up_embed': 6.534}
    for name, (base, spread) in spreads.items():
        noise = np.random.default_rng([zlib.crc32(name.encode()), seed]).standard_normal(out[name].shape)
        drawn = base * np.exp(spread * noise) if base else spread * noise
        out[name] = jnp.asarray(drawn.astype(out[name].dtype))
    for name, factor in factors.items():
        out[name] = (out[name] * factor).astype(out[name].dtype)
    return out
```

```python
from contextlib import ExitStack

import numpy as np
import concourse.bass as bass
from concourse import mybir
from concourse.alu_op_type import AluOpType as ALU

F32 = mybir.dt.float32
F16 = mybir.dt.float16
BF16 = mybir.dt.bfloat16
I32 = mybir.dt.int32
U32 = mybir.dt.uint32
ACT = mybir.ActivationFunctionType
AX = mybir.AxisListType

P = 128
B = 8
N = 512
D = 512
TT = N // P
CC = D // P
H = 16
HD = D // H
LKV = 120
EPS = 1e-5
SELF_SCALE = 1.0 / HD
CROSS_SCALE = float(HD) ** -0.5
CAUSAL_ADD = -10000.0
HUGE = 2.0 ** 60
PAIRS = H // 2
SELF_UNITS = TT * PAIRS
CROSS_UNITS = TT * 2
UNITS = SELF_UNITS + CROSS_UNITS

EH = 4
KEYS = 128
TOPK = 8
EXPERTS = 8192
SEL = EH * TOPK
EROW = 2 * D
LAST = EXPERTS - 1
INTER = 2048
CHUNKS = INTER // P

PIECE = 1024
RING = 6
W_Q, W_K, W_V, W_O, W_K2, W_V2, W_Q2, W_O2, W_FQ = range(0, 18, 2)
W_MLP = 18
PIECES = W_MLP + 3 * (CHUNKS // 2)
assert PIECES % RING == 0
LAPS = PIECES // RING

SLOTS = 16
GATHERS = TT * SEL
NOW = (TT - 1) * SEL
STEPS = 2 * TOPK + 2
TILE_STEPS = EH * STEPS

SELF_END = SELF_UNITS + 7


def deferred_steps(u):
    counts = [1] * 16 + [2] * 8 + [3] * 8 + [2] * 8
    first = sum(counts[:u])
    return range(first, first + counts[u])


def at(b, per_batch, k):
    return b * per_batch + k


def earlier(b):
    return not (isinstance(b, int) and b == 0)


def decoder_layer(nc, x_tok, x_feat, ctx_feat, pieces, keys, table, rows, cols, consts, out, NB=B):
    with ExitStack() as ctx:
        def sb(name, shape, dt=F32):
            return ctx.enter_context(nc.sbuf_tensor(name, shape, dt))

        def ps(name, shape):
            return ctx.enter_context(nc.psum_tensor(name, shape, F32))

        def sem(name):
            return ctx.enter_context(nc.semaphore(name))

        identf = sb("identf", [P, P])
        rotate = sb("rotate", [P, P])
        cos = sb("cos", [P, N])
        sin = sb("sin", [P, N])
        iota8 = sb("iota8", [P, TOPK])
        identh = sb("identh", [P, P], F16)
        maskh = sb("maskh", [P, P], F16)
        identb = sb("identb", [P, P], BF16)
        maskb = sb("maskb", [P, LKV], BF16)
        keysT = sb("keysT", [P, 2, 2, KEYS])
        bo_all = sb("bo_all", [P, D])
        bo2_all = sb("bo2_all", [P, D])
        bv2_all = sb("bv2_all", [P, D])
        last_down = sb("last_down", [P, D])
        last_up = sb("last_up", [P, D])
        bcols = sb("bcols", [P, 2, CC])
        bq_scaled = sb("bq_scaled", [P, CC])
        ring = sb("ring", [P, RING, PIECE])
        xres = sb("xres", [P, TT, D])
        xT = sb("xT", [P, CC, N])
        actT = sb("actT", [P, CC, N])
        ctxT = sb("ctxT", [P, CC, LKV])
        qT = sb("qT", [P, CC, N])
        kT = sb("kT", [P, CC, N])
        vp = sb("vp", [P, 2 * TT * D])
        vtok = vp[:, 0:TT * D].rearrange("p (t f) -> p t f", t=TT)
        prob = vp[:, TT * D:2 * TT * D].rearrange("p (b h k) -> p b h k", b=2, h=2)
        sims = vp[:, :].rearrange("p (t j m k) -> p t j m k", t=TT, j=2, m=4)
        pT = sb("pT", [P, 2, 2, 512])
        qk0 = pT[:, 0]
        k2T = sb("k2T", [P, CC, LKV])
        v2 = sb("v2", [P, D])
        anorm = sb("anorm", [P, D])
        anormT = sb("anormT", [P, CC, P])
        rot = [anorm[:, :], anormT[:, :, :].rearrange("p c k -> p (c k)")]
        x2 = sb("x2", [P, TT, D])
        y3 = sb("y3", [P, TT, D])
        gate = [qT[:, 0], qT[:, 1]]
        hid = [qT[:, 2], qT[:, 3]]
        rowsG = sb("rowsG", [P, SLOTS, EROW])
        nmax = sb("nmax", [P, 2, 8])
        rsum = sb("rsum", [P, 2, H])
        rinv = sb("rinv", [P, H])
        stats = sb("stats", [P, 6])
        mv = sb("mv", [P, 2])
        veps = sb("veps", [P, 1])
        rstd = sb("rstd", [P, 1])
        rtmp = sb("rtmp", [P, 1])
        top1 = sb("top1", [P, 2, EH, TOPK])
        top1i = sb("top1i", [P, 2 * EH * TOPK], U32)
        top1f = sb("top1f", [P, 2 * EH, TOPK])
        sums = sb("sums", [P, EH, TOPK, TOPK])
        best = sb("best", [P, EH, TOPK])
        besti = sb("besti", [P, SEL], U32)
        parts = sb("parts", [P, 2, SEL], U32)
        partf = sb("partf", [P, 2 * SEL])
        onehot = sb("onehot", [P, 2 * SEL, TOPK])
        picked = sb("picked", [P, 2, SEL])
        idxf = sb("idxf", [P, SEL])
        shifted = sb("shifted", [P, EH, TOPK])
        expo = sb("expo", [P, EH, TOPK])
        esum = sb("esum", [P, EH])
        einv = sb("einv", [P, EH])
        last_dot = sb("last_dot", [P, 1])
        invalid = sb("invalid", [P, SEL])
        idx = sb("idx", [P, TT, SEL], U32)
        valid = sb("valid", [P, TT, SEL])
        wlast = sb("wlast", [P, TT, SEL])
        soft = sb("soft", [P, TT, SEL])
        dots = sb("dots", [P, TT, SEL])
        act_in = sb("act_in", [P, TT, SEL])
        act_out = sb("act_out", [P, TT, SEL])
        gall = sb("gall", [P, TT, SEL])
        gvalid = sb("gvalid", [P, TT, SEL])
        glast = sb("glast", [P, TT, SEL])
        glsum = sb("glsum", [P, 1])

        S = [ps("S0", [P, 2, 512]), ps("S1", [P, 2, 512])]
        T = ps("T", [P, 2, 512])
        O = ps("O", [P, 512])
        M = ps("M", [P, 512])
        accs = [S[0][:, 0], S[0][:, 1], S[1][:, 0], S[1][:, 1]]
        gu_banks = [(T[:, 0], T[:, 1]), (O[:, :], M[:, :])]
        rot_banks = [O[:, :], M[:, :]]

        const_in, const_ready, rows_clear = sem("const_in"), sem("const_ready"), sem("rows_clear")
        w_in = [sem(f"w_in{i}") for i in range(RING)]
        x_in, xT_in, ctx_in = sem("x_in"), sem("xT_in"), sem("ctx_in")
        row_in = [sem(f"row_in{i}") for i in range(SLOTS)]
        out_done = [sem(f"out_done{i}") for i in range(TT)]
        proj_done, rot_done, s_done, t_done, pv_done = (sem(n) for n in (
            "proj_done", "rot_done", "s_done", "t_done", "pv_done"))
        at_done, oproj_done, xt_done, kv2_done, q2_done = (sem(n) for n in (
            "at_done", "oproj_done", "xt_done", "kv2_done", "q2_done"))
        qf_done, sim_done, gu_done, down_done = (sem(n) for n in ("qf_done", "sim_done", "gu_done", "down_done"))
        qk0_ready, v_ready, k2_ready, p_ready = sem("qk0_ready"), sem("v_ready"), sem("k2_ready"), sem("p_ready")
        pt_ready, at_ready, xt_ready, q2_ready = sem("pt_ready"), sem("at_ready"), sem("xt_ready"), sem("q2_ready")
        qf_ready, sim_ready, gate_ready = sem("qf_ready"), sem("sim_ready"), sem("gate_ready")
        expo_ready, silu_ready = sem("expo_ready"), sem("silu_ready")
        rot_used, rope_ready, nmax_ready, an_ready = sem("rot_used"), sem("rope_ready"), sem("nmax_ready"), sem("an_ready")
        y_ready, xn_ready, v2_ready, hid_ready = sem("y_ready"), sem("xn_ready"), sem("v2_ready"), sem("hid_ready")
        acc_taken, shifted_ready, idx_ready = sem("acc_taken"), sem("shifted_ready"), sem("idx_ready")
        act_in_ready, rows_used, out_ready = sem("act_in_ready"), sem("rows_used"), sem("out_ready")
        xb_ready, xb2_ready, cosq_ready = sem("xb_ready"), sem("xb2_ready"), sem("cosq_ready")
        dve_chain, dve_gate, pool_gate = sem("dve_chain"), sem("dve_gate"), sem("pool_gate")

        block = ctx.enter_context(nc.Block())
        NCONST = 15

        @block.sync
        def _(sp):
            for dst, src in ((identf[:, :], consts[:, 0:128]), (rotate[:, :], consts[:, 128:256]),
                             (cos[:, :], consts[:, 256:768]), (sin[:, :], consts[:, 768:1280]),
                             (vp[:, 0:128], consts[:, 1280:1408]), (vp[:, 128:128 + LKV], consts[:, 1408:1408 + LKV]),
                             (iota8[:, :], consts[:, 1536:1544]),
                             (keysT[:, :, :, :].rearrange("p a m k -> p (a m k)"), keys),
                             (bo_all[:, :], rows[0:1, :].to_broadcast([P, D])),
                             (bo2_all[:, :], rows[1:2, :].to_broadcast([P, D])),
                             (bv2_all[:, :], rows[2:3, :].to_broadcast([P, D])),
                             (last_down[:, :], table[LAST:EXPERTS, 0:D].to_broadcast([P, D])),
                             (last_up[:, :], table[LAST:EXPERTS, D:EROW].to_broadcast([P, D])),
                             (bcols[:, 0, :], cols[:, 0:CC]), (bcols[:, 1, :], cols[:, CC:2 * CC])):
                sp.dma_start(dst, src).then_inc(const_in, 16)

            def load(k):
                sp.dma_start(ring[:, k % RING, :], pieces[k]).then_inc(w_in[k % RING], 16)

            def batch(b):
                if earlier(b):
                    sp.wait_ge(proj_done, at(b, 12, 0))
                sp.dma_start(xT[:, :, :], x_feat[b]).then_inc(xT_in, 16)
                if earlier(b):
                    sp.wait_ge(y_ready, at(b, 8, 0))
                sp.dma_start(xres[:, :, :], x_tok[b]).then_inc(x_in, 16)
                if earlier(b):
                    sp.wait_ge(kv2_done, at(b, 2, 0))
                sp.dma_start(ctxT[:, :, :], ctx_feat[b]).then_inc(ctx_in, 16)
                for k in range(RING):
                    if earlier(b) and k % 3 < 2:
                        sp.wait_ge(gu_done, at(b, CHUNKS, 2 * (k // 3) - 2))
                    if earlier(b) and k % 3 == 2:
                        sp.wait_ge(down_done, at(b, CHUNKS, 2 * (k // 3) - 2))
                    load(k)
                for h in range(4):
                    sp.wait_ge(proj_done, at(b, 12, 2 * h + 2))
                    load(W_O + h)
                sp.wait_ge(proj_done, at(b, 12, 12))
                load(W_V2)
                load(W_V2 + 1)
                sp.wait_ge(oproj_done, at(b, 8, TT))
                load(W_Q2)
                load(W_Q2 + 1)
                sp.wait_ge(kv2_done, at(b, 2, 2))
                for k in range(W_O2, W_MLP):
                    load(k)
                for h in range(2):
                    sp.wait_ge(q2_done, at(b, CC, 2 * h + 2))
                    load(W_MLP + h)
                sp.wait_ge(oproj_done, at(b, 8, 8))
                load(W_MLP + 2)
                load(W_MLP + 3)
                for h in range(2):
                    sp.wait_ge(qf_done, at(b, CC, 2 * h + 2))
                    load(W_MLP + 4 + h)
                for g in range(2, CHUNKS // 2):
                    sp.wait_ge(gu_done, at(b, CHUNKS, 2 * g - 2))
                    load(W_MLP + 3 * g)
                    load(W_MLP + 3 * g + 1)
                    sp.wait_ge(down_done, at(b, CHUNKS, 2 * g - 2))
                    load(W_MLP + 3 * g + 2)

            batch(0)
            with sp.Fori(1, NB) as b:
                batch(b)
            for t in range(TT):
                sp.wait_ge(out_done[t], 16 * NB)

        @block.tensor
        def _(pe):
            mm = nc.tensor.matmul

            def weights(b, k):
                pe.wait_ge(w_in[k % RING], at(b, 16 * LAPS, 16 * (k // RING + 1)))
                return ring[:, k % RING, :].rearrange("p (c f) -> p c f", c=CC)

            def by_feature(b, dst, piece, j, rhs):
                w = weights(b, piece + j // 2)
                for c in range(CC):
                    last = mm(dst, lhsT=w[:, c, (j % 2) * P:(j % 2 + 1) * P], rhs=rhs[:, c, :],
                              start=(c == 0), stop=(c == CC - 1))
                return last

            def by_token(b, dst, piece, lhs):
                for h in range(2):
                    w = weights(b, piece + h)
                    for c in range(CC):
                        last = mm(dst[:, h * 256:(h + 1) * 256], lhsT=lhs[:, c, :], rhs=w[:, c, :],
                                  start=(c == 0), stop=(c == CC - 1))
                return last

            def project_qk(b, i):
                if i == 0:
                    pe.wait_ge(xT_in, at(b, 16, 16))
                if i < 2:
                    if earlier(b):
                        pe.wait_ge(hid_ready, at(b, CHUNKS, -1))
                else:
                    pe.wait_ge(qk0_ready, at(b, 8, i - 1))
                by_feature(b, T[:, i % 2], W_Q if i < 4 else W_K, i % 4, xT).then_inc(proj_done, 1)

            def rotate_qk(b, i):
                pe.wait_ge(qk0_ready, at(b, 8, i + 1))
                if i < 2:
                    if earlier(b):
                        pe.wait_ge(hid_ready, at(b, CHUNKS, 0))
                else:
                    pe.wait_ge(rot_used, at(b, 8, i - 1))
                mm(rot_banks[i % 2], lhsT=rotate[:, :], rhs=qk0[:, i % 2, :], start=True, stop=True).then_inc(rot_done, 1)

            def project_v(b, t):
                if t < 2:
                    pe.wait_ge(qk0_ready, at(b, 8, 7 + t))
                else:
                    pe.wait_ge(v_ready, at(b, TT, t - 1))
                by_token(b, T[:, t % 2], W_V, xT[:, :, t * P:(t + 1) * P]).then_inc(proj_done, 1)

            def self_scores(b, u):
                t, p = divmod(u, PAIRS)
                width = (t + 1) * P
                if u == 0:
                    pe.wait_ge(rope_ready, at(b, 8, 8))
                    if earlier(b):
                        pe.wait_ge(acc_taken, at(b, TT, 0))
                if u >= 2:
                    pe.wait_ge(p_ready, at(b, UNITS, u - 1))
                for hh in range(2):
                    r = 64 * (p % 2) + 32 * hh
                    q = qT[r:r + 32, p // 2, t * P:width]
                    if t > 0:
                        mm(S[u % 2][:, hh, 0:t * P], lhsT=q, rhs=kT[r:r + 32, p // 2, 0:t * P], start=True, stop=True)
                    mm(S[u % 2][:, hh, t * P:width], lhsT=q, rhs=kT[r:r + 32, p // 2, t * P:width], start=True, stop=False)
                for hh in range(2):
                    last = mm(S[u % 2][:, hh, t * P:width], lhsT=identh[:, :], rhs=maskh[:, :], start=False, stop=True)
                last.then_inc(s_done, 1)

            def self_turn(b, u):
                t = u // PAIRS
                pe.wait_ge(p_ready, at(b, UNITS, u + 1))
                for hh in range(2):
                    if u == 0:
                        pe.wait_ge(v_ready, at(b, TT, TT))
                    else:
                        pe.wait_ge(pt_ready, at(b, 2 * UNITS, 2 * (u - 1) + hh + 1))
                    for k in range(t + 1):
                        last = nc.tensor.transpose(T[:, hh, k * P:(k + 1) * P], prob[:, u % 2, hh, k * P:(k + 1) * P],
                                                   identf[:, :])
                    last.then_inc(t_done, 1)

            def self_values(b, u):
                t, p = divmod(u, PAIRS)
                if p == 0 and t > 0:
                    pe.wait_ge(an_ready, at(b, 8, t))
                for hh in range(2):
                    h = 2 * p + hh
                    pe.wait_ge(pt_ready, at(b, 2 * UNITS, 2 * u + hh + 1))
                    for k in range(t + 1):
                        last = mm(O[:, h * HD:(h + 1) * HD], lhsT=pT[:, u % 2, hh, k * P:(k + 1) * P],
                                  rhs=vtok[:, k, h * HD:(h + 1) * HD], start=(k == 0), stop=(k == t))
                last.then_inc(pv_done, 1)

            def turn_attention(b, n):
                pe.wait_ge(an_ready, at(b, 8, n + 1))
                if 0 < n <= TT:
                    pe.wait_ge(xt_ready, at(b, 8, n))
                if n > TT:
                    pe.wait_ge(y_ready, at(b, 8, n))
                for c in range(CC):
                    last = nc.tensor.transpose(M[:, c * P:(c + 1) * P], anorm[:, c * P:(c + 1) * P], identf[:, :])
                last.then_inc(at_done, 1)

            def project_out(b, n):
                pe.wait_ge(at_ready, at(b, 8, n + 1))
                by_token(b, M[:, :], W_O if n < TT else W_O2, anormT).then_inc(oproj_done, 1)

            def turn_norm(b, n):
                pe.wait_ge(xn_ready, at(b, 8, n + 1))
                src = xres[:, n, :] if n < TT else x2[:, n - TT, :]
                dst = M[:, :] if n < TT else accs[n - TT]
                for c in range(CC):
                    last = nc.tensor.transpose(dst[:, c * P:(c + 1) * P], src[:, c * P:(c + 1) * P], identf[:, :])
                last.then_inc(xt_done, 1)

            def project_k2(b):
                pe.wait_ge(ctx_in, at(b, 16, 16))
                pe.wait_ge(pt_ready, at(b, 2 * UNITS, 2 * SELF_UNITS - 1))
                for j in range(CC):
                    last = by_feature(b, T[:, 0, j * LKV:(j + 1) * LKV], W_K2, j, ctxT)
                last.then_inc(kv2_done, 1)

            def project_v2(b):
                pe.wait_ge(pt_ready, at(b, 2 * UNITS, 2 * SELF_UNITS))
                by_token(b, T[0:LKV, 1], W_V2, ctxT).then_inc(kv2_done, 1)

            def project_q2(b, j):
                if j == 0:
                    pe.wait_ge(xt_ready, at(b, 8, TT))
                by_feature(b, accs[j], W_Q2, j, actT).then_inc(q2_done, 1)

            def cross_scores(b, v):
                t, g = divmod(v, 2)
                if v == 0:
                    pe.wait_ge(q2_ready, at(b, CC, CC))
                    pe.wait_ge(k2_ready, at(b, 1, 1))
                if v >= 2:
                    pe.wait_ge(p_ready, at(b, UNITS, SELF_UNITS + v - 1))
                for c in range(CC):
                    for hh in range(2):
                        r = 64 * g + 32 * hh
                        last = mm(S[v % 2][:, hh, c * LKV:(c + 1) * LKV], lhsT=qT[r:r + 32, c, t * P:(t + 1) * P],
                                  rhs=k2T[r:r + 32, c, :], start=True, stop=(t > 0))
                        if t == 0:
                            last = mm(S[v % 2][:, hh, c * LKV:(c + 1) * LKV], lhsT=identb[:, :], rhs=maskb[:, :],
                                      start=False, stop=True)
                last.then_inc(s_done, 1)

            def cross_turn(b, v):
                u = SELF_UNITS + v
                pe.wait_ge(p_ready, at(b, UNITS, u + 1))
                for hh in range(2):
                    if v == 0:
                        pe.wait_ge(k2_ready if hh == 0 else v2_ready, at(b, 1, 1))
                    else:
                        pe.wait_ge(pt_ready, at(b, 2 * UNITS, 2 * (u - 1) + hh + 1))
                    for c in range(CC):
                        last = nc.tensor.transpose(T[0:LKV, hh, c * P:(c + 1) * P],
                                                   prob[:, v % 2, hh, c * LKV:(c + 1) * LKV], identf[:, :])
                    last.then_inc(t_done, 1)

            def cross_values(b, v):
                t, g = divmod(v, 2)
                u = SELF_UNITS + v
                if g == 0:
                    pe.wait_ge(an_ready, at(b, 8, TT + t))
                for hh in range(2):
                    pe.wait_ge(pt_ready, at(b, 2 * UNITS, 2 * u + hh + 1))
                    for c in range(CC):
                        h = 4 * c + 2 * g + hh
                        last = mm(O[:, h * HD:(h + 1) * HD], lhsT=pT[0:LKV, v % 2, hh, c * P:(c + 1) * P],
                                  rhs=v2[0:LKV, h * HD:(h + 1) * HD], start=True, stop=True)
                last.then_inc(pv_done, 1)

            def project_fq(b, j):
                if j == 0:
                    pe.wait_ge(xt_ready, at(b, 8, 8))
                by_feature(b, (T[:, 0], T[:, 1], O[:, :], M[:, :])[j], W_FQ, j, actT).then_inc(qf_done, 1)

            def similarities(b, t):
                if t == 0:
                    pe.wait_ge(qf_ready, at(b, CC, CC))
                if t >= 2:
                    pe.wait_ge(sim_ready, at(b, TT, t - 1))
                for m in range(4):
                    for j in range(2):
                        last = mm(S[t % 2][:, j, m * KEYS:(m + 1) * KEYS], lhsT=kT[64 * j:64 * j + 64, m, t * P:(t + 1) * P],
                                  rhs=keysT[64 * j:64 * j + 64, m // 2, m % 2, :], start=True, stop=True)
                last.then_inc(sim_done, 1)

            def gate_up(b, k):
                if k >= 2:
                    pe.wait_ge(hid_ready, at(b, CHUNKS, k - 1))
                for side in range(2):
                    w = weights(b, W_MLP + 3 * (k // 2) + side)
                    for c in range(CC):
                        last = mm(gu_banks[k % 2][side], lhsT=w[:, c, (k % 2) * P:(k % 2 + 1) * P], rhs=actT[:, c, :],
                                  start=(c == 0), stop=(c == CC - 1))
                last.then_inc(gu_done, 1)

            def down(b, k):
                weights(b, W_MLP + 3 * (k // 2) + 2)
                w = ring[:, (W_MLP + 3 * (k // 2) + 2) % RING, (k % 2) * D:(k % 2 + 1) * D]
                pe.wait_ge(hid_ready, at(b, CHUNKS, k + 1))
                if k == 0:
                    pe.wait_ge(sim_ready, at(b, TT, TT))
                for t in range(TT):
                    last = mm(accs[t], lhsT=hid[k % 2][:, t * P:(t + 1) * P], rhs=w,
                              start=(k == 0), stop=(k == CHUNKS - 1))
                last.then_inc(down_done, 1)

            def batch(b):
                for i in range(8):
                    project_qk(b, i)
                    if i >= 1:
                        rotate_qk(b, i - 1)
                project_v(b, 0)
                rotate_qk(b, 7)
                for t in range(1, TT):
                    project_v(b, t)
                for u in range(SELF_END):
                    if u < SELF_UNITS:
                        self_scores(b, u)
                    if 1 <= u <= SELF_UNITS:
                        self_turn(b, u - 1)
                    if 2 <= u <= SELF_UNITS + 1:
                        self_values(b, u - 2)
                    if u == SELF_UNITS + 2:
                        project_k2(b)
                    if u == SELF_UNITS + 3:
                        project_v2(b)
                    tile, stage = divmod(u - PAIRS, PAIRS)
                    if stage == 2 and tile >= 0:
                        turn_attention(b, tile)
                    if stage == 3 and tile >= 0:
                        project_out(b, tile)
                    if stage == 6 and tile >= 0:
                        turn_norm(b, tile)
                for j in range(CC):
                    project_q2(b, j)
                for v in range(CROSS_UNITS + 4):
                    if v < CROSS_UNITS:
                        cross_scores(b, v)
                    if 1 <= v <= CROSS_UNITS:
                        cross_turn(b, v - 1)
                    if 2 <= v <= CROSS_UNITS + 1:
                        cross_values(b, v - 2)
                    if v >= 4 and v % 2 == 0:
                        turn_attention(b, TT + v // 2 - 2)
                    if v >= 4 and v % 2 == 1:
                        project_out(b, TT + v // 2 - 2)
                for t in range(TT):
                    turn_norm(b, TT + t)
                for j in range(CC):
                    project_fq(b, j)
                for t in range(TT):
                    similarities(b, t)
                for k in range(CHUNKS):
                    gate_up(b, k)
                    if k >= 1:
                        down(b, k - 1)
                down(b, CHUNKS - 1)

            pe.wait_ge(const_ready, 1)
            batch(0)
            with pe.Fori(1, NB) as b:
                batch(b)

        @block.scalar
        def _(act):
            def copy(dst, src, bias=0.0, scale=1.0):
                return nc.scalar.activation(dst, src, ACT.Identity, bias=bias, scale=scale)

            def expert_silu(b, t, h):
                act.wait_ge(act_in_ready, at(b, TT * EH, t * EH + h + 1))
                part = slice(h * TOPK, (h + 1) * TOPK)
                nc.scalar.activation(act_out[:, t, part], act_in[:, t, part], ACT.Silu).then_inc(silu_ready, 1)

            def deferred(b, u):
                for n in deferred_steps(u):
                    if n % STEPS == TOPK:
                        expert_silu(b - 1, TT - 1, n // STEPS)

            def take_turned(b, u, rows_, width):
                for hh in range(2):
                    act.wait_ge(t_done, at(b, 2 * UNITS, 2 * u + hh + 1))
                    if u >= 2:
                        act.wait_ge(pv_done, at(b, UNITS, u - 1))
                    copy(pT[0:rows_, u % 2, hh, 0:width], T[0:rows_, hh, 0:width]).then_inc(pt_ready, 1)

            def self_exp(b, u):
                t, p = divmod(u, PAIRS)
                width = (t + 1) * P
                act.wait_ge(nmax_ready, at(b, UNITS, u + 1))
                for hh in range(2):
                    h = 2 * p + hh
                    last = nc.scalar.activation(prob[:, u % 2, hh, 0:width], S[u % 2][:, hh, 0:width], ACT.Exp,
                                                bias=nmax[:, u % 2, hh:hh + 1], accum_out=rsum[:, t % 2, h:h + 1])
                last.then_inc(p_ready, 1)

            def cross_exp(b, v):
                t, g = divmod(v, 2)
                act.wait_ge(nmax_ready, at(b, UNITS, SELF_UNITS + v + 1))
                for hh in range(2):
                    for c in range(CC):
                        h = 4 * c + 2 * g + hh
                        last = nc.scalar.activation(prob[:, v % 2, hh, c * LKV:(c + 1) * LKV],
                                                    S[v % 2][:, hh, c * LKV:(c + 1) * LKV], ACT.Exp,
                                                    bias=nmax[:, v % 2, hh * CC + c:hh * CC + c + 1],
                                                    accum_out=rsum[:, t % 2, h:h + 1])
                last.then_inc(p_ready, 1)

            def take_attention(b, n):
                act.wait_ge(at_done, at(b, 8, n + 1))
                copy(anormT[:, :, :].rearrange("p c k -> p (c k)"), M[:, :]).then_inc(at_ready, 1)

            def take_norm(b, n):
                act.wait_ge(xt_done, at(b, 8, n + 1))
                t = n % TT
                src = M[:, :] if n < TT else accs[t]
                copy(actT[:, :, t * P:(t + 1) * P], src.rearrange("p (c k) -> p c k", c=CC)).then_inc(xt_ready, 1)

            def batch(b, first):
                for i in range(8):
                    act.wait_ge(proj_done, at(b, 12, i + 1))
                    if i >= 2:
                        act.wait_ge(rot_done, at(b, 8, i - 1))
                        act.wait_ge(cosq_ready, at(b, 8, i - 1))
                    copy(qk0[:, i % 2, :], T[:, i % 2], scale=SELF_SCALE if i < 4 else 1.0).then_inc(qk0_ready, 1)
                for t in range(TT):
                    act.wait_ge(proj_done, at(b, 12, 9 + t))
                    copy(vtok[:, t, :], T[:, t % 2]).then_inc(v_ready, 1)
                for u in range(SELF_END):
                    if 1 <= u <= SELF_UNITS:
                        take_turned(b, u - 1, P, ((u - 1) // PAIRS + 1) * P)
                    if u < SELF_UNITS:
                        self_exp(b, u)
                        if not first:
                            deferred(b, u)
                    if u == SELF_UNITS + 2:
                        act.wait_ge(kv2_done, at(b, 2, 1))
                        for j in range(CC):
                            last = copy(k2T[:, j, :], T[:, 0, j * LKV:(j + 1) * LKV], bias=bcols[:, 1, j:j + 1])
                        last.then_inc(k2_ready, 1)
                    tile, stage = divmod(u - PAIRS, PAIRS)
                    if stage == 2 and tile >= 0:
                        take_attention(b, tile)
                    if stage == 6 and tile >= 0:
                        take_norm(b, tile)
                for j in range(CC):
                    act.wait_ge(q2_done, at(b, CC, j + 1))
                    copy(qT[:, j, :], accs[j], bias=bq_scaled[:, j:j + 1], scale=CROSS_SCALE).then_inc(q2_ready, 1)
                for v in range(CROSS_UNITS + 4):
                    if 1 <= v <= CROSS_UNITS:
                        take_turned(b, SELF_UNITS + v - 1, LKV, CC * P)
                    if v < CROSS_UNITS:
                        cross_exp(b, v)
                        if not first:
                            deferred(b, SELF_UNITS + v)
                    if v >= 4 and v % 2 == 0:
                        take_attention(b, TT + v // 2 - 2)
                for t in range(TT):
                    take_norm(b, TT + t)
                for j in range(CC):
                    act.wait_ge(qf_done, at(b, CC, j + 1))
                    copy(kT[:, j, :], (T[:, 0], T[:, 1], O[:, :], M[:, :])[j]).then_inc(qf_ready, 1)
                for t in range(TT):
                    act.wait_ge(sim_done, at(b, TT, t + 1))
                    copy(vp[:, t * 1024:(t + 1) * 1024].rearrange("p (j k) -> p j k", j=2), S[t % 2][:, :, :]).then_inc(sim_ready, 1)
                for k in range(CHUNKS):
                    act.wait_ge(gu_done, at(b, CHUNKS, k + 1))
                    if k >= 2:
                        act.wait_ge(hid_ready, at(b, CHUNKS, k - 1))
                    nc.scalar.activation(gate[k % 2], gu_banks[k % 2][0], ACT.Silu).then_inc(gate_ready, 1)
                    if k < TT:
                        act.wait_ge(shifted_ready, at(b, TT, k + 1))
                        nc.scalar.activation(expo[:, :, :], shifted[:, :, :], ACT.Exp).then_inc(expo_ready, 1)
                    else:
                        expert_silu(b, (k - TT) // EH, (k - TT) % EH)

            act.wait_ge(const_ready, 1)
            batch(0, True)
            with act.Fori(1, NB) as b:
                batch(b, False)
            for h in range(EH):
                expert_silu(NB - 1, TT - 1, h)

        @block.vector
        def _(dve):
            count = [0]

            def link(ins):
                count[0] += 1
                ins.then_inc(dve_chain, 1)
                dve.wait_ge(dve_chain, count[0])

            def clear_links():
                dve.sem_clear(dve_chain)
                count[0] = 0

            v = nc.vector
            bc = lambda ap, axis, shape: ap.unsqueeze(axis).to_broadcast(shape)

            def rope(b, i):
                dve.wait_ge(rot_done, at(b, 8, i + 1))
                v.tensor_tensor(rot[i % 2], rot_banks[i % 2], sin[:, :], ALU.mult).then_inc(rot_used, 1)
                dst = (qT if i < 4 else kT)[:, i % 4, :]
                dve.wait_ge(cosq_ready, at(b, 8, i + 1))
                dve.wait_ge(rot_used, at(b, 8, i + 1))
                v.tensor_tensor(dst, dst, rot[i % 2], ALU.add).then_inc(rope_ready, 1)

            def self_max(b, u):
                width = (u // PAIRS + 1) * P
                dve.wait_ge(s_done, at(b, UNITS, u + 1))
                v.tensor_reduce(out=nmax[:, u % 2, 0:2], in_=S[u % 2][:, :, 0:width], axis=AX.X, op=ALU.max,
                                negate=True).then_inc(nmax_ready, 1)

            def cross_max(b, w):
                dve.wait_ge(s_done, at(b, UNITS, SELF_UNITS + w + 1))
                v.tensor_reduce(out=nmax[:, w % 2, 0:8].rearrange("p (h c) -> p h c", h=2),
                                in_=S[w % 2][:, :, 0:CC * LKV].rearrange("p h (c k) -> p h c k", c=CC), axis=AX.X,
                                op=ALU.max, negate=True).then_inc(nmax_ready, 1)

            def divide(b, n):
                dve.wait_ge(pv_done, at(b, UNITS, PAIRS * (n + 1) if n < TT else SELF_UNITS + 2 * (n - TT + 1)))
                link(v.reciprocal(rinv[:, :], rsum[:, n % 2, :]))
                v.tensor_tensor(anorm[:, :].rearrange("p (h d) -> p h d", h=H), O[:, :].rearrange("p (h d) -> p h d", h=H),
                                bc(rinv[:, :], 2, [P, H, HD]), ALU.mult).then_inc(an_ready, 1)

            def layer_norm(src, dst):
                link(v.bn_stats(out=stats[:, :], in_=src))
                link(v.bn_aggr(out=mv[:, :], in_=stats[:, :]))
                link(v.tensor_scalar(veps[:, :], mv[:, 1:2], EPS, None, ALU.add))
                link(v.tensor_scalar(rstd[:, :].bitcast(I32), veps[:, :].bitcast(I32), -0.5, float(0x5F3759DF),
                                     ALU.mult, ALU.add))
                for _ in range(4):
                    link(v.scalar_tensor_tensor(out=rtmp[:, :], in0=rstd[:, :], scalar=veps[:, 0:1], in1=rstd[:, :],
                                                op0=ALU.mult, op1=ALU.mult))
                    link(v.tensor_scalar(rtmp[:, :], rtmp[:, :], -0.5, 1.5, ALU.mult, ALU.add))
                    link(v.tensor_tensor(rstd[:, :], rstd[:, :], rtmp[:, :], ALU.mult))
                return v.tensor_scalar(dst, src, mv[:, 0:1], rstd[:, 0:1], ALU.subtract, ALU.mult)

            def residual_norm(b, n):
                dve.wait_ge(xb_ready if n < TT else xb2_ready, at(b, TT, n % TT + 1))
                dve.wait_ge(oproj_done, at(b, 8, n + 1))
                dst = xres[:, n, :] if n < TT else x2[:, n - TT, :]
                v.tensor_tensor(dst, M[:, :], xres[:, n % TT, :], ALU.add).then_inc(y_ready, 1)
                dve.wait_ge(y_ready, at(b, 8, n + 1))
                layer_norm(dst, dst).then_inc(xn_ready, 1)

            def route(b, t):
                dve.wait_ge(sim_ready, at(b, TT, t + 1))
                link(v.tensor_tensor_reduce(out=anorm[:, :], in0=x2[:, t, :], in1=last_down[:, :],
                                            scale=1.0, scalar=0.0, op0=ALU.mult, op1=ALU.add, accum_out=last_dot[:, :]))
                for half in range(2):
                    for h in range(EH):
                        keysim = sims[:, t, h % 2, 2 * half + h // 2, :]
                        link(v.max(out=top1[:, half, h, :], in_=keysim))
                        place = (half * EH + h) * TOPK
                        last = v.max_index(out=top1i[:, place:place + TOPK], in_max=top1[:, half, h, :], in_values=keysim)
                        if half * EH + h == 2 * EH - 1:
                            link(last)
                link(v.tensor_copy(top1f[:, :, :].rearrange("p a k -> p (a k)"), top1i[:, :]))
                link(v.tensor_tensor(sums[:, :, :, :], bc(top1[:, 0], 3, [P, EH, TOPK, TOPK]),
                                     bc(top1[:, 1], 2, [P, EH, TOPK, TOPK]), ALU.add))
                for h in range(EH):
                    flat = sums[:, h].rearrange("p a c -> p (a c)")
                    link(v.max(out=best[:, h, :], in_=flat))
                    last = v.max_index(out=besti[:, h * TOPK:(h + 1) * TOPK], in_max=best[:, h, :], in_values=flat)
                link(last)
                v.tensor_tensor(shifted[:, :, :], best[:, :, :], best[:, :, 0:1].to_broadcast([P, EH, TOPK]),
                                ALU.subtract).then_inc(shifted_ready, 1)
                v.tensor_scalar(parts[:, 0, :], besti[:, :], 3, None, ALU.logical_shift_right)
                link(v.tensor_scalar(parts[:, 1, :], besti[:, :], 7, None, ALU.bitwise_and))
                link(v.tensor_copy(partf[:, :], parts[:, :, :].rearrange("p a k -> p (a k)")))
                link(v.tensor_tensor(onehot[:, :, :], bc(partf[:, :], 2, [P, 2 * SEL, TOPK]),
                                     bc(iota8[:, :], 1, [P, 2 * SEL, TOPK]), ALU.is_equal))
                spread = onehot[:, :, :].rearrange("p (a k) c -> p a k c", k=TOPK)
                link(v.tensor_tensor(spread, spread, bc(top1f[:, :, :], 2, [P, 2 * EH, TOPK, TOPK]), ALU.mult))
                link(v.tensor_reduce(out=picked[:, :, :].rearrange("p a k -> p (a k)"), in_=onehot[:, :, :], axis=AX.X,
                                     op=ALU.add))
                link(v.scalar_tensor_tensor(out=idxf[:, :], in0=picked[:, 0, :], scalar=float(KEYS), in1=picked[:, 1, :],
                                            op0=ALU.mult, op1=ALU.add))
                v.tensor_copy(idx[:, t, :], idxf[:, :]).then_inc(idx_ready, 1)
                v.tensor_scalar(invalid[:, :], idxf[:, :], float(LAST), None, ALU.is_ge)
                link(v.tensor_scalar(valid[:, t, :], idxf[:, :], float(LAST), None, ALU.is_lt))
                link(v.tensor_scalar(wlast[:, t, :], invalid[:, :], last_dot[:, 0:1], None, ALU.mult))
                dve.wait_ge(expo_ready, at(b, TT, t + 1))
                link(v.tensor_reduce(out=esum[:, :], in_=expo[:, :, :], axis=AX.X, op=ALU.add))
                link(v.reciprocal(einv[:, :], esum[:, :]))
                link(v.tensor_tensor(soft[:, t, :].rearrange("p (h k) -> p h k", h=EH), expo[:, :, :],
                                     bc(einv[:, :], 2, [P, EH, TOPK]), ALU.mult))

            def expert_step(b, t, n):
                h, s = divmod(n, STEPS)
                part = slice(h * TOPK, (h + 1) * TOPK)
                if s < TOPK:
                    e = h * TOPK + s
                    g = t * SEL + e
                    dve.wait_ge(row_in[g % SLOTS], at(b, 16 * (GATHERS // SLOTS), 16 * (g // SLOTS + 1)))
                    ins = v.tensor_tensor_reduce(out=rowsG[:, g % SLOTS, 0:D], in0=rowsG[:, g % SLOTS, 0:D],
                                                 in1=x2[:, t, :], scale=1.0, scalar=0.0, op0=ALU.mult, op1=ALU.add,
                                                 accum_out=dots[:, t, e:e + 1])
                    if s == TOPK - 1:
                        link(ins)
                elif s == TOPK:
                    link(v.tensor_tensor(act_in[:, t, part], dots[:, t, part], valid[:, t, part], ALU.mult))
                    v.tensor_tensor(act_in[:, t, part], act_in[:, t, part], wlast[:, t, part],
                                    ALU.add).then_inc(act_in_ready, 1)
                elif s == TOPK + 1:
                    dve.wait_ge(silu_ready, at(b, TT * EH, t * EH + h + 1))
                    link(v.tensor_tensor(gall[:, t, part], act_out[:, t, part], soft[:, t, part], ALU.mult))
                    link(v.tensor_tensor(gvalid[:, t, part], gall[:, t, part], valid[:, t, part], ALU.mult))
                    link(v.tensor_tensor(glast[:, t, part], gall[:, t, part], gvalid[:, t, part], ALU.subtract))
                else:
                    e = h * TOPK + s - TOPK - 2
                    g = t * SEL + e
                    base = y3[:, t, :]
                    if e == 0 and t < TT - 1:
                        base = x2[:, t, :]
                        if earlier(b):
                            dve.wait_ge(out_done[t], at(b, 16, 0))
                    if e % 2 == 0 and e > 0:
                        dve.wait_ge(rows_used, at(b, GATHERS // 2, g // 2))
                    ins = v.scalar_tensor_tensor(out=y3[:, t, :], in0=rowsG[:, g % SLOTS, D:EROW],
                                                 scalar=gvalid[:, t, e:e + 1], in1=base, op0=ALU.mult, op1=ALU.add)
                    if e % 2 == 0:
                        link(ins)
                    else:
                        ins.then_inc(rows_used, 1)

            def finish(b, t):
                link(v.tensor_reduce(out=glsum[:, :], in_=glast[:, t, :], axis=AX.X, op=ALU.add))
                dve.wait_ge(rows_used, at(b, GATHERS // 2, (t + 1) * SEL // 2))
                link(v.scalar_tensor_tensor(out=y3[:, t, :], in0=last_up[:, :], scalar=glsum[:, 0:1], in1=y3[:, t, :],
                                            op0=ALU.mult, op1=ALU.add))
                layer_norm(y3[:, t, :], y3[:, t, :]).then_inc(out_ready, 1)

            def deferred(b, u):
                for n in deferred_steps(u):
                    expert_step(b - 1, TT - 1, n)
                if u == UNITS - 1:
                    finish(b - 1, TT - 1)

            def hidden(b, k):
                dve.wait_ge(gate_ready, at(b, CHUNKS, k + 1))
                if k >= 2:
                    dve.wait_ge(down_done, at(b, CHUNKS, k - 1))
                v.tensor_tensor(hid[k % 2], gate[k % 2], gu_banks[k % 2][1], ALU.mult).then_inc(hid_ready, 1)

            def batch(b, first):
                for i in range(8):
                    rope(b, i)
                for u in range(SELF_END):
                    if u < SELF_UNITS:
                        self_max(b, u)
                        if not first:
                            deferred(b, u)
                    if u == SELF_UNITS + 4:
                        dve.wait_ge(kv2_done, at(b, 2, 2))
                        v.tensor_tensor(v2[0:LKV, :], T[0:LKV, 1], bv2_all[0:LKV, :], ALU.add).then_inc(v2_ready, 1)
                    tile, stage = divmod(u - PAIRS, PAIRS)
                    if stage == 1 and tile >= 0:
                        divide(b, tile)
                    if stage == 4 and tile >= 0:
                        residual_norm(b, tile)
                for w in range(CROSS_UNITS + 5):
                    if w < CROSS_UNITS:
                        cross_max(b, w)
                        if not first:
                            deferred(b, SELF_UNITS + w)
                    if w >= 6 and w % 2 == 0:
                        residual_norm(b, TT + w // 2 - 3)
                    if w >= 3 and w % 2 == 1 and w // 2 - 1 < TT:
                        divide(b, TT + w // 2 - 1)
                for k in range(CHUNKS):
                    if k < TT:
                        route(b, k)
                    else:
                        t, h = divmod(k - TT, EH)
                        for n in range(h * STEPS, (h + 1) * STEPS):
                            expert_step(b, t, n)
                    hidden(b, k)
                dve.wait_ge(down_done, at(b, CHUNKS, CHUNKS))
                dve.wait_ge(rows_used, at(b, GATHERS // 2, NOW // 2))
                for t in range(TT):
                    if t == TT - 1:
                        if earlier(b):
                            dve.wait_ge(out_done[t], at(b, 16, 0))
                    base = y3[:, t, :] if t < TT - 1 else x2[:, t, :]
                    v.tensor_tensor(y3[:, t, :], base, accs[t], ALU.add).then_inc(acc_taken, 1)
                dve.wait_ge(acc_taken, at(b, TT, TT))
                for t in range(TT - 1):
                    finish(b, t)
                clear_links()

            dve.wait_ge(const_in, 16 * NCONST)
            link(v.tensor_copy(identh[:, :], identf[:, :]))
            link(v.tensor_copy(maskh[:, :], vp[:, 0:128]))
            link(v.tensor_scalar(identb[:, :], identf[:, :], HUGE, None, ALU.mult))
            link(v.tensor_copy(maskb[:, :], vp[:, 128:128 + LKV]))
            v.tensor_scalar(bq_scaled[:, :], bcols[:, 0, :], CROSS_SCALE, None, ALU.mult).then_inc(const_ready, 1)
            clear_links()
            batch(0, True)
            with dve.Fori(1, NB) as b:
                batch(b, False)
            for n in range(TILE_STEPS):
                expert_step(NB - 1, TT - 1, n)
            finish(NB - 1, TT - 1)

        @block.gpsimd
        def _(pool):
            g = nc.gpsimd

            def gather(b, n):
                t, e = divmod(n, SEL)
                if n % 2 == 0:
                    if n >= SLOTS or earlier(b):
                        pool.wait_ge(rows_used, at(b, GATHERS // 2, (n - SLOTS) // 2 + 1))
                    if e == 0:
                        pool.wait_ge(idx_ready, at(b, TT, t + 1))
                    pool.sem_inc(pool_gate, 1)
                g.indirect_dma_start(out=rowsG[:, n % SLOTS, :], out_offset=None, in_=table,
                                     in_offset=bass.IndirectOffsetOnAxis(ap=idx[:, t, e:e + 1], axis=0),
                                     bounds_check=LAST - 1, oob_is_err=False).then_inc(row_in[n % SLOTS], 16)

            def store(b, t):
                pool.wait_ge(out_ready, at(b, TT, t + 1))
                pool.sem_inc(pool_gate, 1)
                pool.dma_start(out[b, t], y3[:, t, :]).then_inc(out_done[t], 16)

            def deferred_gathers(b):
                for n in range(NOW + SLOTS, GATHERS):
                    gather(b - 1, n)

            def batch(b, first):
                pool.wait_ge(x_in, at(b, 16, 16))
                for t in range(TT):
                    g.tensor_tensor(xres[:, t, :], xres[:, t, :], bo_all[:, :], ALU.add).then_inc(xb_ready, 1)
                for i in range(8):
                    pool.wait_ge(qk0_ready, at(b, 8, i + 1))
                    g.tensor_tensor((qT if i < 4 else kT)[:, i % 4, :], qk0[:, i % 2, :], cos[:, :],
                                    ALU.mult).then_inc(cosq_ready, 1)
                if not first:
                    deferred_gathers(b)
                for t in range(TT):
                    pool.wait_ge(xt_done, at(b, 8, t + 1))
                    g.tensor_tensor(xres[:, t, :], xres[:, t, :], bo2_all[:, :], ALU.add).then_inc(xb2_ready, 1)
                if not first:
                    store(b - 1, TT - 1)
                for n in range(NOW + SLOTS):
                    gather(b, n)
                for t in range(TT - 1):
                    store(b, t)

            g.memset(rowsG[:, :, :], 0.0).then_inc(rows_clear, 1)
            pool.wait_ge(rows_clear, 1)
            pool.wait_ge(const_in, 16 * NCONST)
            batch(0, True)
            with pool.Fori(1, NB) as b:
                batch(b, False)
            deferred_gathers(NB)
            store(NB - 1, TT - 1)


def _pieces(w):
    wt = w.T.reshape(CC, P, -1)
    n = wt.shape[2] // 256
    return wt.reshape(CC, P, n, 256).transpose(2, 1, 0, 3).reshape(n, P, PIECE)


def _constants():
    c = np.zeros((P, 1544), np.float32)
    i = np.arange(P)
    c[i, i] = 1.0
    even = i[::2]
    c[even + 1, P + even] = -1.0
    c[even, P + even + 1] = 1.0
    inv_freq = (np.float32(1.0) / np.float32(10000.0) ** (np.arange(0, HD, 2, dtype=np.float32) / np.float32(HD)))
    ang = np.arange(N, dtype=np.float32)[None, :] * inv_freq.astype(np.float32)[(i % HD) // 2][:, None]
    c[:, 256:768] = np.cos(ang)
    c[:, 768:1280] = np.sin(ang)
    c[:, 1280:1408] = np.where(i[None, :] > i[:, None], CAUSAL_ADD, 0.0)
    c[:, 1408:1408 + LKV] = np.where(i[None, :LKV] > i[:, None], -HUGE, 0.0)
    c[:, 1536:1544] = np.arange(TOPK)
    return c


def kernel(**inputs):
    import concourse.bacc as _bacc
    from concourse.bass_utils import run_bass_kernel_spmd as _run

    a = {k: np.asarray(v) for k, v in inputs.items()}
    x, c = a["x"], a["ctx_1024"]
    wg, wu = _pieces(a["L0_ffn_Wg"]), _pieces(a["L0_ffn_Wu"])
    wd = a["L0_ffn_Wd"].T.reshape(CHUNKS // 2, 2, P, D).transpose(0, 2, 1, 3).reshape(CHUNKS // 2, P, PIECE)
    pieces = [_pieces(a[n]) for n in ("L0_attn_Wq", "L0_attn_Wk", "L0_attn_Wv", "L0_attn_Wo", "L0_xattn_Wk",
                                      "L0_xattn_Wv", "L0_xattn_Wq", "L0_xattn_Wo", "L0_ffn_Wq")]
    pieces.append(np.stack([wg, wu, wd], axis=1).reshape(-1, P, PIECE))
    arrays = {
        "x_tok": x.reshape(B, TT, P, D).transpose(0, 2, 1, 3),
        "x_feat": x.transpose(0, 2, 1).reshape(B, CC, P, N).transpose(0, 2, 1, 3),
        "ctx_feat": c.transpose(0, 2, 1).reshape(B, CC, P, LKV).transpose(0, 2, 1, 3),
        "pieces": np.concatenate(pieces),
        "keys": a["L0_ffn_keys"].reshape(2, 2, KEYS, 2, 64).transpose(1, 4, 3, 0, 2).reshape(P, 4 * KEYS),
        "table": np.concatenate([a["L0_ffn_down_embed"], a["L0_ffn_up_embed"]], axis=1),
        "rows": np.stack([a["L0_attn_bo"], a["L0_xattn_bo"], a["L0_xattn_bv"]]),
        "cols": np.concatenate([a["L0_xattn_bq"].reshape(CC, P).T, a["L0_xattn_bk"].reshape(CC, P).T], axis=1),
        "consts": _constants(),
    }
    arrays = {f"{k}_dram": np.ascontiguousarray(v) for k, v in arrays.items()}
    nc = _bacc.Bacc("TRN2", target_bir_lowering=False, num_devices=1)
    args = [nc.dram_tensor(k, v.shape, mybir.dt.from_np(v.dtype), kind="ExternalInput").ap() for k, v in arrays.items()]
    out = nc.dram_tensor("out_dram", (B, TT, P, D), F32, kind="ExternalOutput").ap()
    decoder_layer(nc, *args, out)
    r = _run(nc, [arrays], core_ids=[0])
    return r.results[0]["out_dram"].reshape(B, N, D)
```

```python
from contextlib import ExitStack

import numpy as np
import concourse.bass as bass
from concourse import mybir
from concourse.alu_op_type import AluOpType as ALU

F32 = mybir.dt.float32
F16 = mybir.dt.float16
BF16 = mybir.dt.bfloat16
I32 = mybir.dt.int32
U32 = mybir.dt.uint32
ACT = mybir.ActivationFunctionType
AX = mybir.AxisListType

P = 128
B = 8
N = 512
D = 512
TT = N // P
CC = D // P
H = 16
HD = D // H
LKV = 120
EPS = 1e-5
SELF_SCALE = 1.0 / HD
CROSS_SCALE = float(HD) ** -0.5
CAUSAL_ADD = -10000.0
HUGE = 2.0 ** 60
PAIRS = H // 2
SELF_UNITS = TT * PAIRS
CROSS_UNITS = TT * 2
UNITS = SELF_UNITS + CROSS_UNITS

EH = 4
KEYS = 128
TOPK = 8
EXPERTS = 8192
SEL = EH * TOPK
EROW = 2 * D
LAST = EXPERTS - 1
INTER = 2048
CHUNKS = INTER // P

PIECE = 1024
RING = 6
W_Q, W_K, W_V, W_O, W_K2, W_V2, W_Q2, W_O2, W_FQ = range(0, 18, 2)
W_MLP = 18
PIECES = W_MLP + 3 * (CHUNKS // 2)
assert PIECES % RING == 0
LAPS = PIECES // RING

SLOTS = 16
GATHERS = TT * SEL
EUNITS = TT * EH
STEPS = 2 * TOPK + 2
AHEAD = 2
NOW_UNITS = 8
NOW_STEPS = NOW_UNITS * STEPS
NOW = NOW_UNITS * TOPK
MLP_STEPS = NOW_STEPS // (CHUNKS - TT)
assert MLP_STEPS * (CHUNKS - TT) == NOW_STEPS

ROTATIONS = 2 * CC
PLACES = [4] * ROTATIONS + [12] + [1] * 8 + [2] * 8 + [3] * 16 + [4] * 4 + [3] * 4
FIRST_UNIT = ROTATIONS + 1
assert len(PLACES) == FIRST_UNIT + UNITS and sum(PLACES) == (EUNITS - NOW_UNITS) * STEPS

SELF_END = SELF_UNITS + 6


def deferred_steps(place):
    first = NOW_STEPS + sum(PLACES[:place])
    return range(first, first + PLACES[place])


def deferred_finishes(place):
    steps = deferred_steps(place)
    ends = [(t, (t + 1) * EH * STEPS - 1) for t in range(TT)]
    return [t for t, end in ends if end in steps or (end < NOW_STEPS and place == ROTATIONS)]


def mlp_steps(k):
    return range((k - TT) * MLP_STEPS, (k - TT + 1) * MLP_STEPS)


def rows_left(steps):
    unit, s = divmod(steps, STEPS)
    return unit * TOPK + max(0, s - TOPK - 2) // 2 * 2


def deferred_rows(place):
    before = NOW_STEPS + sum(PLACES[:place])
    after = before + PLACES[place]
    return range(min(GATHERS, rows_left(before) + SLOTS), min(GATHERS, rows_left(after) + SLOTS))


def at(b, per_batch, k):
    return b * per_batch + k


def earlier(b):
    return not (isinstance(b, int) and b == 0)


def decoder_layer(nc, x_tok, x_feat, ctx_feat, pieces, keys, table, rows, cols, consts, out, NB=B):
    with ExitStack() as ctx:
        def sb(name, shape, dt=F32):
            return ctx.enter_context(nc.sbuf_tensor(name, shape, dt))

        def ps(name, shape):
            return ctx.enter_context(nc.psum_tensor(name, shape, F32))

        def sem(name):
            return ctx.enter_context(nc.semaphore(name))

        identf = sb("identf", [P, P])
        rotate = sb("rotate", [P, P])
        cos = sb("cos", [P, N])
        sin = sb("sin", [P, N])
        iota8 = sb("iota8", [P, TOPK])
        identh = sb("identh", [P, P], F16)
        maskh = sb("maskh", [P, P], F16)
        identb = sb("identb", [P, P], BF16)
        maskb = sb("maskb", [P, LKV], BF16)
        keysT = sb("keysT", [P, 2, 2, KEYS])
        bo_all = sb("bo_all", [P, D])
        bo2_all = sb("bo2_all", [P, D])
        bv2_all = sb("bv2_all", [P, D])
        last_down = sb("last_down", [P, D])
        last_up = sb("last_up", [P, D])
        bcols = sb("bcols", [P, 2, CC])
        bq_scaled = sb("bq_scaled", [P, CC])
        ring = sb("ring", [P, RING, PIECE])
        xres = sb("xres", [P, TT, D])
        xT = sb("xT", [P, CC, N])
        actT = sb("actT", [P, CC, N])
        ctxT = sb("ctxT", [P, CC, LKV])
        qT = sb("qT", [P, CC, N])
        kT = sb("kT", [P, CC, N])
        vp = sb("vp", [P, 2 * TT * D])
        vtok = vp[:, 0:TT * D].rearrange("p (t f) -> p t f", t=TT)
        prob = vp[:, TT * D:2 * TT * D].rearrange("p (b h k) -> p b h k", b=2, h=2)
        sims = vp[:, :].rearrange("p (t j m k) -> p t j m k", t=TT, j=2, m=4)
        pT = sb("pT", [P, 2, 2, 512])
        qk0 = pT[:, 0]
        k2T = sb("k2T", [P, CC, LKV])
        v2 = sb("v2", [P, D])
        rinvs = sb("rinvs", [P, D])
        attnT = sb("attnT", [P, CC, P])
        rot = [rinvs[:, :], attnT[:, :, :].rearrange("p c k -> p (c k)")]
        x2 = sb("x2", [P, TT, D])
        y3 = sb("y3", [P, TT, D])
        gate = [qT[:, 0], qT[:, 1]]
        hid = [qT[:, 2], qT[:, 3]]
        rowsG = sb("rowsG", [P, SLOTS, EROW])
        nmax = sb("nmax", [P, 2, 8])
        rsum = sb("rsum", [P, 2, H])
        rinv = sb("rinv", [P, H])
        stats = sb("stats", [P, 6])
        mv = sb("mv", [P, 2, 2])
        veps = sb("veps", [P, 1])
        vhalf = sb("vhalf", [P, 1])
        rstd = sb("rstd", [P, 1])
        rtmp = sb("rtmp", [P, 1])
        top1 = sb("top1", [P, 2, EH, TOPK])
        top1i = sb("top1i", [P, 2 * EH * TOPK], U32)
        top1f = sb("top1f", [P, 2 * EH, TOPK])
        sums = sb("sums", [P, EH, TOPK, TOPK])
        best = sb("best", [P, EH, TOPK])
        besti = sb("besti", [P, SEL], U32)
        parts = sb("parts", [P, 2, SEL], U32)
        partf = sb("partf", [P, 2 * SEL])
        onehot = sb("onehot", [P, 2 * SEL, TOPK])
        picked = sb("picked", [P, 2, SEL])
        idxf = sb("idxf", [P, TT, SEL])
        expo = sb("expo", [P, TT, EH, TOPK])
        esum = sb("esum", [P, TT, EH])
        einv = sb("einv", [P, TT, EH])
        last_dot = sb("last_dot", [P, TT])
        idx = sb("idx", [P, TT, SEL], U32)
        valid = sb("valid", [P, TT, SEL])
        wlast = sb("wlast", [P, TT, SEL])
        soft = sb("soft", [P, TT, SEL])
        dots = sb("dots", [P, TT, SEL])
        act_in = sb("act_in", [P, TT, SEL])
        act_out = sb("act_out", [P, TT, SEL])
        gall = sb("gall", [P, TT, SEL])
        gvalid = sb("gvalid", [P, TT, SEL])
        glast = sb("glast", [P, TT, SEL])
        invalid = glast
        glsum = sb("glsum", [P, 1])

        S = [ps("S0", [P, 2, 512]), ps("S1", [P, 2, 512])]
        T = ps("T", [P, 2, 512])
        O = ps("O", [P, 512])
        M = ps("M", [P, 512])
        accs = [S[0][:, 0], S[0][:, 1], S[1][:, 0], S[1][:, 1]]
        gu_banks = [(T[:, 0], T[:, 1]), (O[:, :], M[:, :])]
        rot_banks = [O[:, :], M[:, :]]
        fq_banks = [T[:, 0], T[:, 1], O[:, :], M[:, :]]
        EARLY, LATE = slice(0, N - P), slice(N - P, N)

        const_in, const_ready, rows_clear = sem("const_in"), sem("const_ready"), sem("rows_clear")
        w_in = [sem(f"w_in{i}") for i in range(RING)]
        x_in, xT_in, ctx_in = sem("x_in"), sem("xT_in"), sem("ctx_in")
        row_in = [sem(f"row_in{i}") for i in range(SLOTS)]
        out_done = [sem(f"out_done{i}") for i in range(TT)]
        proj_done, rot_done, s_done, t_done, pv_done = (sem(n) for n in (
            "proj_done", "rot_done", "s_done", "t_done", "pv_done"))
        spread_done, oproj_done, xt_done, kv2_done, q2_done = (sem(n) for n in (
            "spread_done", "oproj_done", "xt_done", "kv2_done", "q2_done"))
        qf_done, sim_done, gu_done, down_done = (sem(n) for n in ("qf_done", "sim_done", "gu_done", "down_done"))
        qk0_ready, v_ready, k2_ready, p_ready = sem("qk0_ready"), sem("v_ready"), sem("k2_ready"), sem("p_ready")
        pt_ready, spread_ready, xt_ready, q2_ready = (sem(n) for n in ("pt_ready", "spread_ready", "xt_ready", "q2_ready"))
        qf_ready, sim_ready, gate_ready = sem("qf_ready"), sem("sim_ready"), sem("gate_ready")
        expo_ready, silu_ready = sem("expo_ready"), sem("silu_ready")
        rot_used, rope_ready, nmax_ready, attn_ready = (sem(n) for n in ("rot_used", "rope_ready", "nmax_ready", "attn_ready"))
        rinv_ready = sem("rinv_ready")
        y_ready, xn_ready, v2_ready, hid_ready = sem("y_ready"), sem("xn_ready"), sem("v2_ready"), sem("hid_ready")
        acc_taken, shifted_ready, idx_ready = sem("acc_taken"), sem("shifted_ready"), sem("idx_ready")
        act_in_ready, rows_used, out_ready = sem("act_in_ready"), sem("rows_used"), sem("out_ready")
        xb_ready, xb2_ready, cosq_ready = sem("xb_ready"), sem("xb2_ready"), sem("cosq_ready")
        dve_chain, dve_gate, pool_gate = sem("dve_chain"), sem("dve_gate"), sem("pool_gate")

        block = ctx.enter_context(nc.Block())
        NCONST = 15

        @block.sync
        def _(sp):
            for dst, src in ((identf[:, :], consts[:, 0:128]), (rotate[:, :], consts[:, 128:256]),
                             (cos[:, :], consts[:, 256:768]), (sin[:, :], consts[:, 768:1280]),
                             (vp[:, 0:128], consts[:, 1280:1408]), (vp[:, 128:128 + LKV], consts[:, 1408:1408 + LKV]),
                             (iota8[:, :], consts[:, 1536:1544]),
                             (keysT[:, :, :, :].rearrange("p a m k -> p (a m k)"), keys),
                             (bo_all[:, :], rows[0:1, :].to_broadcast([P, D])),
                             (bo2_all[:, :], rows[1:2, :].to_broadcast([P, D])),
                             (bv2_all[:, :], rows[2:3, :].to_broadcast([P, D])),
                             (last_down[:, :], table[LAST:EXPERTS, 0:D].to_broadcast([P, D])),
                             (last_up[:, :], table[LAST:EXPERTS, D:EROW].to_broadcast([P, D])),
                             (bcols[:, 0, :], cols[:, 0:CC]), (bcols[:, 1, :], cols[:, CC:2 * CC])):
                sp.dma_start(dst, src).then_inc(const_in, 16)

            def load(k):
                sp.dma_start(ring[:, k % RING, :], pieces[k]).then_inc(w_in[k % RING], 16)

            def batch(b):
                if earlier(b):
                    sp.wait_ge(proj_done, at(b, 12, 0))
                sp.dma_start(xT[:, :, :], x_feat[b]).then_inc(xT_in, 16)
                if earlier(b):
                    sp.wait_ge(y_ready, at(b, 8, 0))
                sp.dma_start(xres[:, :, :], x_tok[b]).then_inc(x_in, 16)
                if earlier(b):
                    sp.wait_ge(kv2_done, at(b, 2, 0))
                sp.dma_start(ctxT[:, :, :], ctx_feat[b]).then_inc(ctx_in, 16)
                for k in range(RING):
                    if earlier(b) and k % 3 < 2:
                        sp.wait_ge(gu_done, at(b, CHUNKS, 2 * (k // 3) - 2))
                    if earlier(b) and k % 3 == 2:
                        sp.wait_ge(down_done, at(b, CHUNKS, 2 * (k // 3) - 2))
                    load(k)
                for h in range(4):
                    sp.wait_ge(proj_done, at(b, 12, 2 * h + 2))
                    load(W_O + h)
                sp.wait_ge(proj_done, at(b, 12, 12))
                load(W_V2)
                load(W_V2 + 1)
                sp.wait_ge(oproj_done, at(b, 8, TT))
                load(W_Q2)
                load(W_Q2 + 1)
                sp.wait_ge(kv2_done, at(b, 2, 2))
                for k in range(W_O2, W_MLP):
                    load(k)
                for h in range(2):
                    sp.wait_ge(q2_done, at(b, CC, 2 * h + 2))
                    load(W_MLP + h)
                sp.wait_ge(oproj_done, at(b, 8, 8))
                load(W_MLP + 2)
                load(W_MLP + 3)
                for h in range(2):
                    sp.wait_ge(qf_done, at(b, CC, 2 * h + 2))
                    load(W_MLP + 4 + h)
                for g in range(2, CHUNKS // 2):
                    sp.wait_ge(gu_done, at(b, CHUNKS, 2 * g - 2))
                    load(W_MLP + 3 * g)
                    load(W_MLP + 3 * g + 1)
                    sp.wait_ge(down_done, at(b, CHUNKS, 2 * g - 2))
                    load(W_MLP + 3 * g + 2)

            batch(0)
            with sp.Fori(1, NB) as b:
                batch(b)
            for t in range(TT):
                sp.wait_ge(out_done[t], 16 * NB)

        @block.tensor
        def _(pe):
            mm = nc.tensor.matmul

            def weights(b, k):
                pe.wait_ge(w_in[k % RING], at(b, 16 * LAPS, 16 * (k // RING + 1)))
                return ring[:, k % RING, :].rearrange("p (c f) -> p c f", c=CC)

            def by_feature(b, dst, piece, j, rhs):
                w = weights(b, piece + j // 2)
                for c in range(CC):
                    last = mm(dst, lhsT=w[:, c, (j % 2) * P:(j % 2 + 1) * P], rhs=rhs[:, c, :],
                              start=(c == 0), stop=(c == CC - 1))
                return last

            def by_token(b, dst, piece, lhs):
                for h in range(2):
                    w = weights(b, piece + h)
                    for c in range(CC):
                        last = mm(dst[:, h * 256:(h + 1) * 256], lhsT=lhs[:, c, :], rhs=w[:, c, :],
                                  start=(c == 0), stop=(c == CC - 1))
                return last

            def project_qk(b, i):
                if i == 0:
                    pe.wait_ge(xT_in, at(b, 16, 16))
                if i < 2:
                    if earlier(b):
                        pe.wait_ge(hid_ready, at(b, CHUNKS, -1))
                else:
                    pe.wait_ge(qk0_ready, at(b, 8, i - 1))
                by_feature(b, T[:, i % 2], W_Q if i < 4 else W_K, i % 4, xT).then_inc(proj_done, 1)

            def rotate_qk(b, i):
                pe.wait_ge(qk0_ready, at(b, 8, i + 1))
                if i < 2:
                    if earlier(b):
                        pe.wait_ge(hid_ready, at(b, CHUNKS, 0))
                else:
                    pe.wait_ge(rot_used, at(b, 8, i - 1))
                mm(rot_banks[i % 2], lhsT=rotate[:, :], rhs=qk0[:, i % 2, :], start=True, stop=True).then_inc(rot_done, 1)

            def project_v(b, t):
                if t < 2:
                    pe.wait_ge(qk0_ready, at(b, 8, 7 + t))
                else:
                    pe.wait_ge(v_ready, at(b, TT, t - 1))
                by_token(b, T[:, t % 2], W_V, xT[:, :, t * P:(t + 1) * P]).then_inc(proj_done, 1)

            def self_scores(b, u):
                t, p = divmod(u, PAIRS)
                width = (t + 1) * P
                if u == 0:
                    pe.wait_ge(rope_ready, at(b, 8, 8))
                    if earlier(b):
                        pe.wait_ge(acc_taken, at(b, TT, 0))
                if u >= 2:
                    pe.wait_ge(p_ready, at(b, UNITS, u - 1))
                for hh in range(2):
                    r = 64 * (p % 2) + 32 * hh
                    q = qT[r:r + 32, p // 2, t * P:width]
                    if t > 0:
                        mm(S[u % 2][:, hh, 0:t * P], lhsT=q, rhs=kT[r:r + 32, p // 2, 0:t * P], start=True, stop=True)
                    mm(S[u % 2][:, hh, t * P:width], lhsT=q, rhs=kT[r:r + 32, p // 2, t * P:width], start=True, stop=False)
                for hh in range(2):
                    last = mm(S[u % 2][:, hh, t * P:width], lhsT=identh[:, :], rhs=maskh[:, :], start=False, stop=True)
                last.then_inc(s_done, 1)

            def self_turn(b, u):
                t = u // PAIRS
                pe.wait_ge(p_ready, at(b, UNITS, u + 1))
                for hh in range(2):
                    if u == 0:
                        pe.wait_ge(v_ready, at(b, TT, TT))
                    else:
                        pe.wait_ge(pt_ready, at(b, 2 * UNITS, 2 * (u - 1) + hh + 1))
                    for k in range(t + 1):
                        last = nc.tensor.transpose(T[:, hh, k * P:(k + 1) * P], prob[:, u % 2, hh, k * P:(k + 1) * P],
                                                   identf[:, :])
                    last.then_inc(t_done, 1)

            def self_values(b, u):
                t, p = divmod(u, PAIRS)
                if p == 0 and t > 0:
                    pe.wait_ge(attn_ready, at(b, 8, t))
                for hh in range(2):
                    h = 2 * p + hh
                    r = 64 * (p % 2) + 32 * hh
                    pe.wait_ge(pt_ready, at(b, 2 * UNITS, 2 * u + hh + 1))
                    for k in range(t + 1):
                        last = mm(O[r:r + HD, (p // 2) * P:(p // 2 + 1) * P], lhsT=vtok[:, k, h * HD:(h + 1) * HD],
                                  rhs=pT[:, u % 2, hh, k * P:(k + 1) * P], start=(k == 0), stop=(k == t))
                last.then_inc(pv_done, 1)

            def spread_sums(b, n):
                pe.wait_ge(rinv_ready, at(b, 8, n + 1))
                if 0 < n <= TT:
                    pe.wait_ge(xt_ready, at(b, 8, n))
                if n > TT:
                    pe.wait_ge(y_ready, at(b, 8, n))
                for c in range(CC):
                    last = nc.tensor.transpose(M[:, c * P:(c + 1) * P], rinvs[:, c * P:(c + 1) * P], identf[:, :])
                last.then_inc(spread_done, 1)

            def project_out(b, n):
                pe.wait_ge(attn_ready, at(b, 8, n + 1))
                by_token(b, M[:, :], W_O if n < TT else W_O2, attnT).then_inc(oproj_done, 1)

            def turn_norm(b, n):
                pe.wait_ge(xn_ready, at(b, 8, n + 1))
                src = xres[:, n, :] if n < TT else x2[:, n - TT, :]
                dst = M[:, :] if n < TT else accs[n - TT]
                for c in range(CC):
                    last = nc.tensor.transpose(dst[:, c * P:(c + 1) * P], src[:, c * P:(c + 1) * P], identf[:, :])
                last.then_inc(xt_done, 1)

            def project_k2(b):
                pe.wait_ge(ctx_in, at(b, 16, 16))
                pe.wait_ge(pt_ready, at(b, 2 * UNITS, 2 * SELF_UNITS - 1))
                for j in range(CC):
                    last = by_feature(b, T[:, 0, j * LKV:(j + 1) * LKV], W_K2, j, ctxT)
                last.then_inc(kv2_done, 1)

            def project_v2(b):
                pe.wait_ge(pt_ready, at(b, 2 * UNITS, 2 * SELF_UNITS))
                by_token(b, T[0:LKV, 1], W_V2, ctxT).then_inc(kv2_done, 1)

            def by_feature_split(b, dst, piece, j, rhs, columns):
                w = weights(b, piece + j // 2)
                for c in range(CC):
                    last = mm(dst[:, columns], lhsT=w[:, c, (j % 2) * P:(j % 2 + 1) * P], rhs=rhs[:, c, columns],
                              start=(c == 0), stop=(c == CC - 1))
                return last

            def project_q2_early(b, j):
                if j == 0:
                    pe.wait_ge(xt_ready, at(b, 8, TT - 1))
                if j == 2:
                    pe.wait_ge(p_ready, at(b, UNITS, SELF_UNITS))
                by_feature_split(b, accs[j], W_Q2, j, actT, EARLY)

            def project_q2_late(b, j):
                if j == 0:
                    pe.wait_ge(xt_ready, at(b, 8, TT))
                by_feature_split(b, accs[j], W_Q2, j, actT, LATE).then_inc(q2_done, 1)

            def cross_scores(b, v):
                t, g = divmod(v, 2)
                if v == 0:
                    pe.wait_ge(q2_ready, at(b, CC, CC))
                    pe.wait_ge(k2_ready, at(b, 1, 1))
                if v >= 2:
                    pe.wait_ge(p_ready, at(b, UNITS, SELF_UNITS + v - 1))
                for c in range(CC):
                    for hh in range(2):
                        r = 64 * g + 32 * hh
                        last = mm(S[v % 2][:, hh, c * LKV:(c + 1) * LKV], lhsT=qT[r:r + 32, c, t * P:(t + 1) * P],
                                  rhs=k2T[r:r + 32, c, :], start=True, stop=(t > 0))
                        if t == 0:
                            last = mm(S[v % 2][:, hh, c * LKV:(c + 1) * LKV], lhsT=identb[:, :], rhs=maskb[:, :],
                                      start=False, stop=True)
                last.then_inc(s_done, 1)

            def cross_turn(b, v):
                u = SELF_UNITS + v
                pe.wait_ge(p_ready, at(b, UNITS, u + 1))
                for hh in range(2):
                    if v == 0:
                        pe.wait_ge(k2_ready if hh == 0 else v2_ready, at(b, 1, 1))
                    else:
                        pe.wait_ge(pt_ready, at(b, 2 * UNITS, 2 * (u - 1) + hh + 1))
                    for c in range(CC):
                        last = nc.tensor.transpose(T[0:LKV, hh, c * P:(c + 1) * P],
                                                   prob[:, v % 2, hh, c * LKV:(c + 1) * LKV], identf[:, :])
                    last.then_inc(t_done, 1)

            def cross_values(b, v):
                t, g = divmod(v, 2)
                u = SELF_UNITS + v
                if g == 0:
                    pe.wait_ge(attn_ready, at(b, 8, TT + t))
                for hh in range(2):
                    pe.wait_ge(pt_ready, at(b, 2 * UNITS, 2 * u + hh + 1))
                    r = 64 * g + 32 * hh
                    for c in range(CC):
                        h = 4 * c + 2 * g + hh
                        last = mm(O[r:r + HD, c * P:(c + 1) * P], lhsT=v2[0:LKV, h * HD:(h + 1) * HD],
                                  rhs=pT[0:LKV, v % 2, hh, c * P:(c + 1) * P], start=True, stop=True)
                last.then_inc(pv_done, 1)

            def project_fq_early(b, j):
                if j == 0:
                    pe.wait_ge(xt_ready, at(b, 8, 8 - 1))
                if j == 3:
                    pe.wait_ge(y_ready, at(b, 8, 8))
                by_feature_split(b, fq_banks[j], W_FQ, j, actT, EARLY)

            def project_fq_late(b, j):
                if j == 0:
                    pe.wait_ge(xt_ready, at(b, 8, 8))
                by_feature_split(b, fq_banks[j], W_FQ, j, actT, LATE).then_inc(qf_done, 1)

            def similarities(b, t):
                if t == 0:
                    pe.wait_ge(qf_ready, at(b, CC, CC))
                if t >= 2:
                    pe.wait_ge(sim_ready, at(b, TT, t - 1))
                for m in range(4):
                    for j in range(2):
                        last = mm(S[t % 2][:, j, m * KEYS:(m + 1) * KEYS], lhsT=kT[64 * j:64 * j + 64, m, t * P:(t + 1) * P],
                                  rhs=keysT[64 * j:64 * j + 64, m // 2, m % 2, :], start=True, stop=True)
                last.then_inc(sim_done, 1)

            def gate_up(b, k):
                if k >= 2:
                    pe.wait_ge(hid_ready, at(b, CHUNKS, k - 1))
                for side in range(2):
                    w = weights(b, W_MLP + 3 * (k // 2) + side)
                    for c in range(CC):
                        last = mm(gu_banks[k % 2][side], lhsT=w[:, c, (k % 2) * P:(k % 2 + 1) * P], rhs=actT[:, c, :],
                                  start=(c == 0), stop=(c == CC - 1))
                last.then_inc(gu_done, 1)

            def down(b, k):
                weights(b, W_MLP + 3 * (k // 2) + 2)
                w = ring[:, (W_MLP + 3 * (k // 2) + 2) % RING, (k % 2) * D:(k % 2 + 1) * D]
                pe.wait_ge(hid_ready, at(b, CHUNKS, k + 1))
                if k == 0:
                    pe.wait_ge(sim_ready, at(b, TT, TT))
                for t in range(TT):
                    last = mm(accs[t], lhsT=hid[k % 2][:, t * P:(t + 1) * P], rhs=w,
                              start=(k == 0), stop=(k == CHUNKS - 1))
                last.then_inc(down_done, 1)

            def batch(b):
                for i in range(8):
                    project_qk(b, i)
                    if i >= 1:
                        rotate_qk(b, i - 1)
                project_v(b, 0)
                rotate_qk(b, 7)
                for t in range(1, TT):
                    project_v(b, t)
                for u in range(SELF_END):
                    tile, stage = divmod(u - PAIRS, PAIRS)
                    if u < SELF_UNITS:
                        self_scores(b, u)
                    if 1 <= u <= SELF_UNITS:
                        self_turn(b, u - 1)
                    if stage == 1 and tile >= 0:
                        spread_sums(b, tile)
                    if 2 <= u <= SELF_UNITS + 1:
                        self_values(b, u - 2)
                    if u == SELF_UNITS + 2:
                        project_k2(b)
                    if stage == 3 and tile >= 0:
                        project_out(b, tile)
                    if u == SELF_UNITS + 3:
                        project_v2(b)
                    if stage == 6 and tile >= 0:
                        turn_norm(b, tile)
                for j in range(CC):
                    project_q2_early(b, j)
                turn_norm(b, TT - 1)
                for j in range(CC):
                    project_q2_late(b, j)
                for v in range(CROSS_UNITS + 3):
                    if v < CROSS_UNITS:
                        cross_scores(b, v)
                    if 1 <= v <= CROSS_UNITS:
                        cross_turn(b, v - 1)
                    if v >= 3 and v % 2 == 1:
                        spread_sums(b, TT + v // 2 - 1)
                    if 2 <= v <= CROSS_UNITS + 1:
                        cross_values(b, v - 2)
                    if v >= 4 and v % 2 == 0:
                        project_out(b, TT + v // 2 - 2)
                for t in range(TT - 1):
                    turn_norm(b, TT + t)
                for j in range(CC):
                    project_fq_early(b, j)
                turn_norm(b, 2 * TT - 1)
                for j in range(CC):
                    project_fq_late(b, j)
                for t in range(TT):
                    similarities(b, t)
                for k in range(CHUNKS):
                    gate_up(b, k)
                    if k >= 1:
                        down(b, k - 1)
                down(b, CHUNKS - 1)

            pe.wait_ge(const_ready, 1)
            batch(0)
            with pe.Fori(1, NB) as b:
                batch(b)

        @block.scalar
        def _(act):
            def copy(dst, src, bias=0.0, scale=1.0):
                return nc.scalar.activation(dst, src, ACT.Identity, bias=bias, scale=scale)

            def expert_silu(b, q):
                t, h = divmod(q, EH)
                act.wait_ge(act_in_ready, at(b, EUNITS, q + 1))
                part = slice(h * TOPK, (h + 1) * TOPK)
                if q < NOW_UNITS:
                    nc.scalar.activation(act_out[:, t, part], act_in[:, t, part], ACT.Silu).then_inc(silu_ready, 1)
                else:
                    nc.scalar.activation(act_out[:, t, part], act_in[:, t, part], ACT.Exp, scale=-1.0).then_inc(silu_ready, 1)

            def expert_silus(b, steps):
                for n in steps:
                    if n % STEPS == TOPK - AHEAD:
                        expert_silu(b, n // STEPS)

            def take_turned(b, u, rows_, width):
                for hh in range(2):
                    act.wait_ge(t_done, at(b, 2 * UNITS, 2 * u + hh + 1))
                    if u >= 2:
                        act.wait_ge(pv_done, at(b, UNITS, u - 1))
                    copy(pT[0:rows_, u % 2, hh, 0:width], T[0:rows_, hh, 0:width]).then_inc(pt_ready, 1)

            def self_exp(b, u):
                t, p = divmod(u, PAIRS)
                width = (t + 1) * P
                act.wait_ge(nmax_ready, at(b, UNITS, u + 1))
                for hh in range(2):
                    h = 2 * p + hh
                    last = nc.scalar.activation(prob[:, u % 2, hh, 0:width], S[u % 2][:, hh, 0:width], ACT.Exp,
                                                bias=nmax[:, u % 2, hh:hh + 1], accum_out=rsum[:, t % 2, h:h + 1])
                last.then_inc(p_ready, 1)

            def cross_exp(b, v):
                t, g = divmod(v, 2)
                act.wait_ge(nmax_ready, at(b, UNITS, SELF_UNITS + v + 1))
                for hh in range(2):
                    for c in range(CC):
                        h = 4 * c + 2 * g + hh
                        last = nc.scalar.activation(prob[:, v % 2, hh, c * LKV:(c + 1) * LKV],
                                                    S[v % 2][:, hh, c * LKV:(c + 1) * LKV], ACT.Exp,
                                                    bias=nmax[:, v % 2, hh * CC + c:hh * CC + c + 1],
                                                    accum_out=rsum[:, t % 2, h:h + 1])
                last.then_inc(p_ready, 1)

            def take_spread(b, n):
                act.wait_ge(spread_done, at(b, 8, n + 1))
                copy(rinvs[:, :], M[:, :]).then_inc(spread_ready, 1)

            def take_norm(b, n):
                act.wait_ge(xt_done, at(b, 8, n + 1))
                t = n % TT
                src = M[:, :] if n < TT else accs[t]
                copy(actT[:, :, t * P:(t + 1) * P], src.rearrange("p (c k) -> p c k", c=CC)).then_inc(xt_ready, 1)

            def batch(b, first):
                for i in range(8):
                    act.wait_ge(proj_done, at(b, 12, i + 1))
                    if i >= 2:
                        act.wait_ge(rot_done, at(b, 8, i - 1))
                        act.wait_ge(cosq_ready, at(b, 8, i - 1))
                    copy(qk0[:, i % 2, :], T[:, i % 2], scale=SELF_SCALE if i < 4 else 1.0).then_inc(qk0_ready, 1)
                    if not first and i >= 1:
                        expert_silus(b - 1, deferred_steps(i - 1))
                for t in range(TT):
                    act.wait_ge(proj_done, at(b, 12, 9 + t))
                    copy(vtok[:, t, :], T[:, t % 2]).then_inc(v_ready, 1)
                    if not first and t == 0:
                        expert_silus(b - 1, deferred_steps(ROTATIONS - 1))
                if not first:
                    expert_silus(b - 1, deferred_steps(ROTATIONS))
                for u in range(SELF_END):
                    if 1 <= u <= SELF_UNITS:
                        take_turned(b, u - 1, P, ((u - 1) // PAIRS + 1) * P)
                    if u < SELF_UNITS:
                        self_exp(b, u)
                    tile, stage = divmod(u - PAIRS, PAIRS)
                    if stage == 1 and tile >= 0:
                        take_spread(b, tile)
                    if u < SELF_UNITS and not first:
                        expert_silus(b - 1, deferred_steps(FIRST_UNIT + u))
                    if u == SELF_UNITS + 2:
                        act.wait_ge(kv2_done, at(b, 2, 1))
                        for j in range(CC):
                            last = copy(k2T[:, j, :], T[:, 0, j * LKV:(j + 1) * LKV], bias=bcols[:, 1, j:j + 1])
                        last.then_inc(k2_ready, 1)
                    if stage == 6 and tile >= 0:
                        take_norm(b, tile)
                take_norm(b, TT - 1)
                for j in range(CC):
                    act.wait_ge(q2_done, at(b, CC, j + 1))
                    copy(qT[:, j, :], accs[j], bias=bq_scaled[:, j:j + 1], scale=CROSS_SCALE).then_inc(q2_ready, 1)
                for v in range(CROSS_UNITS + 2):
                    if 1 <= v <= CROSS_UNITS:
                        take_turned(b, SELF_UNITS + v - 1, LKV, CC * P)
                    if v < CROSS_UNITS:
                        cross_exp(b, v)
                    if v >= 3 and v % 2 == 1:
                        take_spread(b, TT + v // 2 - 1)
                    if v < CROSS_UNITS and not first:
                        expert_silus(b - 1, deferred_steps(FIRST_UNIT + SELF_UNITS + v))
                for t in range(TT):
                    take_norm(b, TT + t)
                for j in range(CC):
                    act.wait_ge(qf_done, at(b, CC, j + 1))
                    copy(kT[:, j, :], fq_banks[j]).then_inc(qf_ready, 1)
                for t in range(TT):
                    act.wait_ge(sim_done, at(b, TT, t + 1))
                    copy(vp[:, t * 1024:(t + 1) * 1024].rearrange("p (j k) -> p j k", j=2), S[t % 2][:, :, :]).then_inc(sim_ready, 1)
                for k in range(CHUNKS):
                    act.wait_ge(gu_done, at(b, CHUNKS, k + 1))
                    if k >= 2:
                        act.wait_ge(hid_ready, at(b, CHUNKS, k - 1))
                    nc.scalar.activation(gate[k % 2], gu_banks[k % 2][0], ACT.Silu).then_inc(gate_ready, 1)
                    if k == TT - 1:
                        act.wait_ge(shifted_ready, at(b, TT, TT))
                        nc.scalar.activation(expo[:, :, :, :], expo[:, :, :, :], ACT.Exp).then_inc(expo_ready, 1)
                    if k >= TT:
                        expert_silus(b, mlp_steps(k))

            act.wait_ge(const_ready, 1)
            batch(0, True)
            with act.Fori(1, NB) as b:
                batch(b, False)
            for q in range(NOW_UNITS, EUNITS):
                expert_silu(NB - 1, q)

        @block.vector
        def _(dve):
            count = [0]

            def link(ins):
                mark(ins)
                dve.wait_ge(dve_chain, count[0])

            def mark(ins):
                count[0] += 1
                ins.then_inc(dve_chain, 1)

            def clear_links():
                dve.sem_clear(dve_chain)
                count[0] = 0

            v = nc.vector
            bc = lambda ap, axis, shape: ap.unsqueeze(axis).to_broadcast(shape)

            def rope(b, i):
                dve.wait_ge(rot_done, at(b, 8, i + 1))
                v.tensor_tensor(rot[i % 2], rot_banks[i % 2], sin[:, :], ALU.mult).then_inc(rot_used, 1)
                dst = (qT if i < 4 else kT)[:, i % 4, :]
                dve.wait_ge(cosq_ready, at(b, 8, i + 1))
                dve.wait_ge(rot_used, at(b, 8, i + 1))
                v.tensor_tensor(dst, dst, rot[i % 2], ALU.add).then_inc(rope_ready, 1)

            def self_max(b, u):
                width = (u // PAIRS + 1) * P
                dve.wait_ge(s_done, at(b, UNITS, u + 1))
                v.tensor_reduce(out=nmax[:, u % 2, 0:2], in_=S[u % 2][:, :, 0:width], axis=AX.X, op=ALU.max,
                                negate=True).then_inc(nmax_ready, 1)

            def cross_max(b, w):
                dve.wait_ge(s_done, at(b, UNITS, SELF_UNITS + w + 1))
                v.tensor_reduce(out=nmax[:, w % 2, 0:8].rearrange("p (h c) -> p h c", h=2),
                                in_=S[w % 2][:, :, 0:CC * LKV].rearrange("p h (c k) -> p h c k", c=CC), axis=AX.X,
                                op=ALU.max, negate=True).then_inc(nmax_ready, 1)

            def invert_sums(b, n):
                dve.wait_ge(p_ready, at(b, UNITS, PAIRS * (n + 1) if n < TT else SELF_UNITS + 2 * (n - TT + 1)))
                link(v.reciprocal(rinv[:, :], rsum[:, n % 2, :]))
                v.tensor_copy(rinvs[:, :].rearrange("p (h d) -> p h d", h=H),
                              bc(rinv[:, :], 2, [P, H, HD])).then_inc(rinv_ready, 1)

            def divide(b, n):
                dve.wait_ge(pv_done, at(b, UNITS, PAIRS * (n + 1) if n < TT else SELF_UNITS + 2 * (n - TT + 1)))
                dve.wait_ge(spread_ready, at(b, 8, n + 1))
                v.tensor_tensor(attnT[:, :, :].rearrange("p c k -> p (c k)"), O[:, :], rinvs[:, :],
                                ALU.mult).then_inc(attn_ready, 1)

            def norm_stats(src, which):
                link(v.bn_stats(out=stats[:, :], in_=src))
                link(v.bn_aggr(out=mv[:, which, :], in_=stats[:, :]))

            def norm_apply(src, dst, which):
                mark(v.tensor_scalar(vhalf[:, :], mv[:, which, 1:2], -0.5, -0.5 * EPS, ALU.mult, ALU.add))
                link(v.tensor_scalar(veps[:, :], mv[:, which, 1:2], EPS, None, ALU.add))
                link(v.tensor_scalar(rstd[:, :].bitcast(I32), veps[:, :].bitcast(I32), -0.5, float(0x5F3759DF),
                                     ALU.mult, ALU.add))
                for _ in range(3):
                    link(v.scalar_tensor_tensor(out=rtmp[:, :], in0=rstd[:, :], scalar=vhalf[:, 0:1], in1=rstd[:, :],
                                                op0=ALU.mult, op1=ALU.mult))
                    link(v.scalar_tensor_tensor(out=rstd[:, :], in0=rtmp[:, :], scalar=1.5, in1=rstd[:, :],
                                                op0=ALU.add, op1=ALU.mult))
                return v.tensor_scalar(dst, src, mv[:, which, 0:1], rstd[:, 0:1], ALU.subtract, ALU.mult)

            def residual_sum(b, n):
                dve.wait_ge(xb_ready if n < TT else xb2_ready, at(b, TT, n % TT + 1))
                dve.wait_ge(oproj_done, at(b, 8, n + 1))
                dst = xres[:, n, :] if n < TT else x2[:, n - TT, :]
                v.tensor_tensor(dst, M[:, :], xres[:, n % TT, :], ALU.add).then_inc(y_ready, 1)
                dve.wait_ge(y_ready, at(b, 8, n + 1))
                norm_stats(dst, 0)

            def residual_norm(b, n):
                dst = xres[:, n, :] if n < TT else x2[:, n - TT, :]
                norm_apply(dst, dst, 0).then_inc(xn_ready, 1)

            def route(b, t):
                dve.wait_ge(sim_ready, at(b, TT, t + 1))
                link(v.tensor_tensor_reduce(out=rinvs[:, :], in0=x2[:, t, :], in1=last_down[:, :],
                                            scale=1.0, scalar=0.0, op0=ALU.mult, op1=ALU.add,
                                            accum_out=last_dot[:, t:t + 1]))
                for half in range(2):
                    for h in range(EH):
                        keysim = sims[:, t, h % 2, 2 * half + h // 2, :]
                        link(v.max(out=top1[:, half, h, :], in_=keysim))
                        place = (half * EH + h) * TOPK
                        last = v.max_index(out=top1i[:, place:place + TOPK], in_max=top1[:, half, h, :], in_values=keysim)
                        if half * EH + h == 2 * EH - 1:
                            link(last)
                link(v.tensor_copy(top1f[:, :, :].rearrange("p a k -> p (a k)"), top1i[:, :]))
                link(v.tensor_tensor(sums[:, :, :, :], bc(top1[:, 0], 3, [P, EH, TOPK, TOPK]),
                                     bc(top1[:, 1], 2, [P, EH, TOPK, TOPK]), ALU.add))
                for h in range(EH):
                    flat = sums[:, h].rearrange("p a c -> p (a c)")
                    link(v.max(out=best[:, h, :], in_=flat))
                    last = v.max_index(out=besti[:, h * TOPK:(h + 1) * TOPK], in_max=best[:, h, :], in_values=flat)
                link(last)
                v.tensor_tensor(expo[:, t, :, :], best[:, :, :], best[:, :, 0:1].to_broadcast([P, EH, TOPK]),
                                ALU.subtract).then_inc(shifted_ready, 1)
                v.tensor_scalar(parts[:, 0, :], besti[:, :], 3, None, ALU.logical_shift_right)
                link(v.tensor_scalar(parts[:, 1, :], besti[:, :], 7, None, ALU.bitwise_and))
                link(v.tensor_copy(partf[:, :], parts[:, :, :].rearrange("p a k -> p (a k)")))
                link(v.tensor_tensor(onehot[:, :, :], bc(partf[:, :], 2, [P, 2 * SEL, TOPK]),
                                     bc(iota8[:, :], 1, [P, 2 * SEL, TOPK]), ALU.is_equal))
                spread = onehot[:, :, :].rearrange("p (a k) c -> p a k c", k=TOPK)
                link(v.tensor_tensor(spread, spread, bc(top1f[:, :, :], 2, [P, 2 * EH, TOPK, TOPK]), ALU.mult))
                link(v.tensor_reduce(out=picked[:, :, :].rearrange("p a k -> p (a k)"), in_=onehot[:, :, :], axis=AX.X,
                                     op=ALU.add))
                link(v.scalar_tensor_tensor(out=idxf[:, t, :], in0=picked[:, 0, :], scalar=float(KEYS), in1=picked[:, 1, :],
                                            op0=ALU.mult, op1=ALU.add))
                v.tensor_copy(idx[:, t, :], idxf[:, t, :]).then_inc(idx_ready, 1)

            def route_weights(b):
                mark(v.tensor_scalar(invalid[:, :, :], idxf[:, :, :], float(LAST), None, ALU.is_ge))
                link(v.tensor_scalar(valid[:, :, :], idxf[:, :, :], float(LAST), None, ALU.is_lt))
                mark(v.tensor_tensor(wlast[:, :, :], invalid[:, :, :], bc(last_dot[:, :], 2, [P, TT, SEL]), ALU.mult))
                dve.wait_ge(expo_ready, at(b, 1, 1))
                flat = expo[:, :, :, :].rearrange("p t h k -> p (t h) k")
                link(v.tensor_reduce(out=esum[:, :, :].rearrange("p t h -> p (t h)"), in_=flat, axis=AX.X, op=ALU.add))
                link(v.reciprocal(einv[:, :, :], esum[:, :, :]))
                link(v.tensor_tensor(soft[:, :, :].rearrange("p t (h k) -> p (t h) k", k=TOPK), flat,
                                     bc(einv[:, :, :].rearrange("p t h -> p (t h)"), 2, [P, TT * EH, TOPK]), ALU.mult))

            def dot(b, q, e):
                t = q // EH
                g = q * TOPK + e
                e += q % EH * TOPK
                dve.wait_ge(row_in[g % SLOTS], at(b, 16 * (GATHERS // SLOTS), 16 * (g // SLOTS + 1)))
                return v.tensor_tensor_reduce(out=rowsG[:, g % SLOTS, 0:D], in0=rowsG[:, g % SLOTS, 0:D],
                                              in1=x2[:, t, :], scale=1.0, scalar=0.0, op0=ALU.mult, op1=ALU.add,
                                              accum_out=dots[:, t, e:e + 1])

            def expert_step(b, n):
                q, s = divmod(n, STEPS)
                t, h = divmod(q, EH)
                part = slice(h * TOPK, (h + 1) * TOPK)
                if s < TOPK - AHEAD:
                    ins = dot(b, q, s + AHEAD)
                    if s == TOPK - AHEAD - 1:
                        link(ins)
                elif s == TOPK - AHEAD:
                    link(v.tensor_tensor(act_in[:, t, part], dots[:, t, part], valid[:, t, part], ALU.mult))
                    v.tensor_tensor(act_in[:, t, part], act_in[:, t, part], wlast[:, t, part],
                                    ALU.add).then_inc(act_in_ready, 1)
                elif s <= TOPK:
                    if q + 1 < EUNITS:
                        dot(b, q + 1, s - TOPK + AHEAD - 1)
                elif s == TOPK + 1:
                    dve.wait_ge(silu_ready, at(b, EUNITS, q + 1))
                    if q < NOW_UNITS:
                        link(v.tensor_tensor(gall[:, t, part], act_out[:, t, part], soft[:, t, part], ALU.mult))
                    else:
                        mark(v.tensor_tensor(gall[:, t, part], act_in[:, t, part], soft[:, t, part], ALU.mult))
                        link(v.tensor_scalar(act_out[:, t, part], act_out[:, t, part], 1.0, None, ALU.add))
                        link(v.reciprocal(act_out[:, t, part], act_out[:, t, part]))
                        link(v.tensor_tensor(gall[:, t, part], gall[:, t, part], act_out[:, t, part], ALU.mult))
                    link(v.tensor_tensor(gvalid[:, t, part], gall[:, t, part], valid[:, t, part], ALU.mult))
                    mark(v.tensor_tensor(glast[:, t, part], gall[:, t, part], gvalid[:, t, part], ALU.subtract))
                else:
                    e = s - TOPK - 2
                    g = q * TOPK + e
                    e += h * TOPK
                    base = y3[:, t, :]
                    if e == 0 and q < NOW_UNITS:
                        base = x2[:, t, :]
                        if earlier(b):
                            dve.wait_ge(out_done[t], at(b, 16, 0))
                    if e % 2 == 0 and e > 0:
                        dve.wait_ge(rows_used, at(b, GATHERS // 2, g // 2))
                    ins = v.scalar_tensor_tensor(out=y3[:, t, :], in0=rowsG[:, g % SLOTS, D:EROW],
                                                 scalar=gvalid[:, t, e:e + 1], in1=base, op0=ALU.mult, op1=ALU.add)
                    if e % 2 == 0:
                        link(ins)
                    else:
                        ins.then_inc(rows_used, 1)

            def finish(b, t):
                link(v.tensor_reduce(out=glsum[:, :], in_=glast[:, t, :], axis=AX.X, op=ALU.add))
                dve.wait_ge(rows_used, at(b, GATHERS // 2, (t + 1) * SEL // 2))
                link(v.scalar_tensor_tensor(out=y3[:, t, :], in0=last_up[:, :], scalar=glsum[:, 0:1], in1=y3[:, t, :],
                                            op0=ALU.mult, op1=ALU.add))
                norm_stats(y3[:, t, :], 1)
                norm_apply(y3[:, t, :], y3[:, t, :], 1).then_inc(out_ready, 1)

            def deferred(b, place):
                for n in deferred_steps(place):
                    expert_step(b - 1, n)
                for t in deferred_finishes(place):
                    finish(b - 1, t)

            def hidden(b, k):
                dve.wait_ge(gate_ready, at(b, CHUNKS, k + 1))
                if k >= 2:
                    dve.wait_ge(down_done, at(b, CHUNKS, k - 1))
                v.tensor_tensor(hid[k % 2], gate[k % 2], gu_banks[k % 2][1], ALU.mult).then_inc(hid_ready, 1)

            def batch(b, first):
                if not first:
                    dve.wait_ge(acc_taken, at(b, TT, 0))
                for i in range(ROTATIONS):
                    rope(b, i)
                    if not first:
                        deferred(b, i)
                if not first:
                    deferred(b, ROTATIONS)
                for u in range(SELF_END):
                    if u < SELF_UNITS:
                        self_max(b, u)
                    tile, stage = divmod(u - PAIRS, PAIRS)
                    if stage == 0 and tile >= 0:
                        invert_sums(b, tile)
                    if stage == 1 and tile >= 0:
                        divide(b, tile)
                    if stage == 4 and tile >= 0:
                        residual_sum(b, tile)
                    if stage == 5 and tile >= 0:
                        residual_norm(b, tile)
                    if u == SELF_UNITS + 5:
                        dve.wait_ge(kv2_done, at(b, 2, 2))
                        v.tensor_tensor(v2[0:LKV, :], T[0:LKV, 1], bv2_all[0:LKV, :], ALU.add).then_inc(v2_ready, 1)
                    if u < SELF_UNITS and not first:
                        deferred(b, FIRST_UNIT + u)
                for w in range(CROSS_UNITS + 5):
                    if w < CROSS_UNITS:
                        cross_max(b, w)
                    if w >= 5 and w % 2 == 1:
                        residual_sum(b, TT + w // 2 - 2)
                    if w >= 2 and w % 2 == 0 and w // 2 - 1 < TT:
                        invert_sums(b, TT + w // 2 - 1)
                    if w >= 3 and w % 2 == 1 and w // 2 - 1 < TT:
                        divide(b, TT + w // 2 - 1)
                    if w >= 6 and w % 2 == 0:
                        residual_norm(b, TT + w // 2 - 3)
                    if w < CROSS_UNITS and not first:
                        deferred(b, FIRST_UNIT + SELF_UNITS + w)
                for k in range(CHUNKS):
                    if k < TT:
                        route(b, k)
                    if k == TT:
                        for e in range(AHEAD):
                            dot(b, 0, e)
                        route_weights(b)
                    if k >= TT:
                        for n in mlp_steps(k):
                            expert_step(b, n)
                    hidden(b, k)
                clear_links()
                dve.wait_ge(down_done, at(b, CHUNKS, CHUNKS))
                dve.wait_ge(rows_used, at(b, GATHERS // 2, NOW // 2))
                for t in range(TT):
                    begun = t * EH < NOW_UNITS
                    if not begun and earlier(b):
                        dve.wait_ge(out_done[t], at(b, 16, 0))
                    v.tensor_tensor(y3[:, t, :], y3[:, t, :] if begun else x2[:, t, :], accs[t],
                                    ALU.add).then_inc(acc_taken, 1)

            dve.wait_ge(const_in, 16 * NCONST)
            link(v.tensor_copy(identh[:, :], identf[:, :]))
            link(v.tensor_copy(maskh[:, :], vp[:, 0:128]))
            link(v.tensor_scalar(identb[:, :], identf[:, :], HUGE, None, ALU.mult))
            link(v.tensor_copy(maskb[:, :], vp[:, 128:128 + LKV]))
            v.tensor_scalar(bq_scaled[:, :], bcols[:, 0, :], CROSS_SCALE, None, ALU.mult).then_inc(const_ready, 1)
            clear_links()
            batch(0, True)
            with dve.Fori(1, NB) as b:
                batch(b, False)
            dve.wait_ge(acc_taken, at(NB, TT, 0))
            for place in range(len(PLACES)):
                deferred(NB, place)

        @block.gpsimd
        def _(pool):
            g = nc.gpsimd

            def gather(b, n):
                t, e = divmod(n, SEL)
                if n % 2 == 0:
                    if n >= SLOTS or earlier(b):
                        pool.wait_ge(rows_used, at(b, GATHERS // 2, (n - SLOTS) // 2 + 1))
                    if e == 0:
                        pool.wait_ge(idx_ready, at(b, TT, t + 1))
                    pool.sem_inc(pool_gate, 1)
                g.indirect_dma_start(out=rowsG[:, n % SLOTS, :], out_offset=None, in_=table,
                                     in_offset=bass.IndirectOffsetOnAxis(ap=idx[:, t, e:e + 1], axis=0),
                                     bounds_check=LAST - 1, oob_is_err=False).then_inc(row_in[n % SLOTS], 16)

            def store(b, t):
                pool.wait_ge(out_ready, at(b, TT, t + 1))
                pool.sem_inc(pool_gate, 1)
                pool.dma_start(out[b, t], y3[:, t, :]).then_inc(out_done[t], 16)

            def deferred(b, place):
                for n in deferred_rows(place):
                    gather(b - 1, n)
                for t in deferred_finishes(place):
                    store(b - 1, t)

            def batch(b, first):
                pool.wait_ge(x_in, at(b, 16, 16))
                for t in range(TT):
                    g.tensor_tensor(xres[:, t, :], xres[:, t, :], bo_all[:, :], ALU.add).then_inc(xb_ready, 1)
                for i in range(ROTATIONS):
                    pool.wait_ge(qk0_ready, at(b, 8, i + 1))
                    g.tensor_tensor((qT if i < 4 else kT)[:, i % 4, :], qk0[:, i % 2, :], cos[:, :],
                                    ALU.mult).then_inc(cosq_ready, 1)
                    if not first and i >= 1:
                        deferred(b, i - 1)
                if not first:
                    for place in range(ROTATIONS - 1, FIRST_UNIT + SELF_UNITS):
                        deferred(b, place)
                for t in range(TT):
                    pool.wait_ge(xt_done, at(b, 8, t + 1))
                    g.tensor_tensor(xres[:, t, :], xres[:, t, :], bo2_all[:, :], ALU.add).then_inc(xb2_ready, 1)
                if not first:
                    for place in range(FIRST_UNIT + SELF_UNITS, len(PLACES)):
                        deferred(b, place)
                for n in range(NOW + SLOTS):
                    gather(b, n)

            g.memset(rowsG[:, :, :], 0.0).then_inc(rows_clear, 1)
            pool.wait_ge(rows_clear, 1)
            pool.wait_ge(const_in, 16 * NCONST)
            batch(0, True)
            with pool.Fori(1, NB) as b:
                batch(b, False)
            for place in range(len(PLACES)):
                deferred(NB, place)


def _pieces(w):
    wt = w.T.reshape(CC, P, -1)
    n = wt.shape[2] // 256
    return wt.reshape(CC, P, n, 256).transpose(2, 1, 0, 3).reshape(n, P, PIECE)


def _constants():
    c = np.zeros((P, 1544), np.float32)
    i = np.arange(P)
    c[i, i] = 1.0
    even = i[::2]
    c[even + 1, P + even] = -1.0
    c[even, P + even + 1] = 1.0
    inv_freq = (np.float32(1.0) / np.float32(10000.0) ** (np.arange(0, HD, 2, dtype=np.float32) / np.float32(HD)))
    ang = np.arange(N, dtype=np.float32)[None, :] * inv_freq.astype(np.float32)[(i % HD) // 2][:, None]
    c[:, 256:768] = np.cos(ang)
    c[:, 768:1280] = np.sin(ang)
    c[:, 1280:1408] = np.where(i[None, :] > i[:, None], CAUSAL_ADD, 0.0)
    c[:, 1408:1408 + LKV] = np.where(i[None, :LKV] > i[:, None], -HUGE, 0.0)
    c[:, 1536:1544] = np.arange(TOPK)
    return c


def kernel(**inputs):
    import concourse.bacc as _bacc
    from concourse.bass_utils import run_bass_kernel_spmd as _run

    a = {k: np.asarray(v) for k, v in inputs.items()}
    x, c = a["x"], a["ctx_1024"]
    wg, wu = _pieces(a["L0_ffn_Wg"]), _pieces(a["L0_ffn_Wu"])
    wd = a["L0_ffn_Wd"].T.reshape(CHUNKS // 2, 2, P, D).transpose(0, 2, 1, 3).reshape(CHUNKS // 2, P, PIECE)
    pieces = [_pieces(a[n]) for n in ("L0_attn_Wq", "L0_attn_Wk", "L0_attn_Wv", "L0_attn_Wo", "L0_xattn_Wk",
                                      "L0_xattn_Wv", "L0_xattn_Wq", "L0_xattn_Wo", "L0_ffn_Wq")]
    pieces.append(np.stack([wg, wu, wd], axis=1).reshape(-1, P, PIECE))
    arrays = {
        "x_tok": x.reshape(B, TT, P, D).transpose(0, 2, 1, 3),
        "x_feat": x.transpose(0, 2, 1).reshape(B, CC, P, N).transpose(0, 2, 1, 3),
        "ctx_feat": c.transpose(0, 2, 1).reshape(B, CC, P, LKV).transpose(0, 2, 1, 3),
        "pieces": np.concatenate(pieces),
        "keys": a["L0_ffn_keys"].reshape(2, 2, KEYS, 2, 64).transpose(1, 4, 3, 0, 2).reshape(P, 4 * KEYS),
        "table": np.concatenate([a["L0_ffn_down_embed"], a["L0_ffn_up_embed"]], axis=1),
        "rows": np.stack([a["L0_attn_bo"], a["L0_xattn_bo"], a["L0_xattn_bv"]]),
        "cols": np.concatenate([a["L0_xattn_bq"].reshape(CC, P).T, a["L0_xattn_bk"].reshape(CC, P).T], axis=1),
        "consts": _constants(),
    }
    arrays = {f"{k}_dram": np.ascontiguousarray(v) for k, v in arrays.items()}
    nc = _bacc.Bacc("TRN2", target_bir_lowering=False, num_devices=1)
    args = [nc.dram_tensor(k, v.shape, mybir.dt.from_np(v.dtype), kind="ExternalInput").ap() for k, v in arrays.items()]
    out = nc.dram_tensor("out_dram", (B, TT, P, D), F32, kind="ExternalOutput").ap()
    decoder_layer(nc, *args, out)
    r = _run(nc, [arrays], core_ids=[0])
    return r.results[0]["out_dram"].reshape(B, N, D)
```

```python
from contextlib import ExitStack

import numpy as np
import concourse.bass as bass
from concourse import mybir
from concourse.alu_op_type import AluOpType as ALU

F32 = mybir.dt.float32
F16 = mybir.dt.float16
BF16 = mybir.dt.bfloat16
I32 = mybir.dt.int32
U32 = mybir.dt.uint32
ACT = mybir.ActivationFunctionType
AX = mybir.AxisListType

P = 128
B = 8
N = 512
D = 512
TT = N // P
CC = D // P
H = 16
HD = D // H
LKV = 120
EPS = 1e-5
SELF_SCALE = 1.0 / HD
CROSS_SCALE = float(HD) ** -0.5
CAUSAL_ADD = -10000.0
HUGE = 2.0 ** 60
PAIRS = H // 2
SELF_UNITS = TT * PAIRS
CROSS_UNITS = TT * 2
UNITS = SELF_UNITS + CROSS_UNITS

EH = 4
KEYS = 128
TOPK = 8
EXPERTS = 8192
SEL = EH * TOPK
EROW = 2 * D
LAST = EXPERTS - 1
INTER = 2048
CHUNKS = INTER // P

PIECE = 1024
RING = 6
W_Q, W_K, W_V, W_O, W_K2, W_Q2, W_V2, W_O2, W_FQ = range(0, 18, 2)
W_MLP = 18
PIECES = W_MLP + 3 * (CHUNKS // 2)
assert PIECES % RING == 0
LAPS = PIECES // RING

SLOTS = 16
GATHERS = TT * SEL
EUNITS = TT * EH
STEPS = 2 * TOPK + 2
AHEAD = 2
NOW_UNITS = 8
NOW_STEPS = NOW_UNITS * STEPS
NOW = NOW_UNITS * TOPK
MLP_STEPS = [12] * 2 + [13] * 8 + [10, 6]
assert len(MLP_STEPS) == CHUNKS - TT and sum(MLP_STEPS) == NOW_STEPS

ROTATIONS = 2 * CC
PLACES = ([9]
          + [3] * 2 + [4] * 6 + [2]
          + [0, 2, 2, 2, 2, 2, 2, 2]
          + [1, 1, 1, 5, 0, 0, 1, 1]
          + [1, 2, 2, 4, 0, 1, 2, 2]
          + [2, 3, 3, 5, 0, 1, 3, 4]
          + [9, 11, 6]
          + [1, 2, 2, 2, 5, 2, 3, 1])
START, FIRST_ROTATION = 0, 1
BESIDE_V = FIRST_ROTATION + ROTATIONS
FIRST_SELF = BESIDE_V + 1
BESIDE_OUT = FIRST_SELF + SELF_UNITS
BESIDE_NORM, BESIDE_Q2 = BESIDE_OUT + 1, BESIDE_OUT + 2
FIRST_CROSS = BESIDE_Q2 + 1
assert len(PLACES) == FIRST_CROSS + CROSS_UNITS and sum(PLACES) == (EUNITS - NOW_UNITS) * STEPS
assert PLACES[START] <= TOPK + 1

SELF_END = SELF_UNITS + 6


def deferred_steps(place):
    first = NOW_STEPS + sum(PLACES[:place])
    return range(first, first + PLACES[place])


def cross_tile(i):
    return (i + 1) % TT


def mlp_steps(k):
    first = sum(MLP_STEPS[:k - TT])
    return range(first, first + MLP_STEPS[k - TT])


def rows_left(steps):
    unit, s = divmod(steps, STEPS)
    return unit * TOPK + max(0, s - TOPK - 2) // 2 * 2


def deferred_rows(place):
    before = NOW_STEPS + sum(PLACES[:place])
    after = before + PLACES[place]
    return range(min(GATHERS, rows_left(before) + SLOTS), min(GATHERS, rows_left(after) + SLOTS))


def at(b, per_batch, k):
    return b * per_batch + k


def earlier(b):
    return not (isinstance(b, int) and b == 0)


def decoder_layer(nc, x_tok, x_feat, ctx_feat, pieces, keys, table, rows, cols, consts, out, NB=B):
    with ExitStack() as ctx:
        def sb(name, shape, dt=F32):
            return ctx.enter_context(nc.sbuf_tensor(name, shape, dt))

        def ps(name, shape):
            return ctx.enter_context(nc.psum_tensor(name, shape, F32))

        def sem(name):
            return ctx.enter_context(nc.semaphore(name))

        identf = sb("identf", [P, P])
        rotate = sb("rotate", [P, P])
        cos = sb("cos", [P, N])
        sin = sb("sin", [P, N])
        iota8 = sb("iota8", [P, TOPK])
        identh = sb("identh", [P, P], F16)
        maskh = sb("maskh", [P, P], F16)
        identb = sb("identb", [P, P], BF16)
        maskb = sb("maskb", [P, LKV], BF16)
        keysT = sb("keysT", [P, 2, 2, KEYS])
        bo_all = sb("bo_all", [P, D])
        bo2_all = sb("bo2_all", [P, D])
        bv2_all = sb("bv2_all", [P, D])
        last_down = sb("last_down", [P, D])
        last_up = sb("last_up", [P, D])
        bcols = sb("bcols", [P, 2, CC])
        bq_scaled = sb("bq_scaled", [P, CC])
        ring = sb("ring", [P, RING, PIECE])
        xres = sb("xres", [P, TT, D])
        xT = sb("xT", [P, CC, N])
        actT = sb("actT", [P, CC, N])
        ctxT = sb("ctxT", [P, CC, LKV])
        qT = sb("qT", [P, CC, N])
        kT = sb("kT", [P, CC, N])
        vp = sb("vp", [P, 2 * TT * D])
        vtok = vp[:, 0:TT * D].rearrange("p (t f) -> p t f", t=TT)
        prob = vp[:, TT * D:2 * TT * D].rearrange("p (b h k) -> p b h k", b=2, h=2)
        sims = vp[:, :].rearrange("p (t j m k) -> p t j m k", t=TT, j=2, m=4)
        pT = sb("pT", [P, 2, 2, 512])
        qk0 = pT[:, 0]
        k2T = sb("k2T", [P, CC, LKV])
        v2 = sb("v2", [P, D])
        rinvs = sb("rinvs", [P, D])
        attnT = sb("attnT", [P, CC, P])
        rot = [rinvs[:, :], attnT[:, :, :].rearrange("p c k -> p (c k)")]
        x2 = sb("x2", [P, TT, D])
        y3 = sb("y3", [P, TT, D])
        gate = [qT[:, 0], qT[:, 1]]
        hid = [qT[:, 2], qT[:, 3]]
        diags = qT[:, :, :].rearrange("p c (e k) -> p (c e) k", k=P).rearrange("p (u e) k -> p u e k", u=2)
        rowsG = sb("rowsG", [P, SLOTS, EROW])
        nmax = sb("nmax", [P, 2, 8])
        rsum = sb("rsum", [P, 2, H])
        rinv = sb("rinv", [P, H])
        stats = sb("stats", [P, 6])
        mv = sb("mv", [P, TT, 2])
        veps = sb("veps", [P, TT])
        vhalf = sb("vhalf", [P, TT])
        rstd = sb("rstd", [P, TT])
        rtmp = sb("rtmp", [P, TT])
        top1 = sb("top1", [P, 2, EH, TOPK])
        top1i = sb("top1i", [P, 2 * EH * TOPK], U32)
        top1f = sb("top1f", [P, 2 * EH, TOPK])
        sums = sb("sums", [P, EH, TOPK, TOPK])
        best = sb("best", [P, EH, TOPK])
        besti = sb("besti", [P, SEL], U32)
        parts = sb("parts", [P, 2, SEL], U32)
        partf = sb("partf", [P, 2 * SEL])
        onehot = sb("onehot", [P, 2 * SEL, TOPK])
        picked = sb("picked", [P, 2, SEL])
        idxf = sb("idxf", [P, TT, SEL])
        expo = sb("expo", [P, TT, EH, TOPK])
        esum = sb("esum", [P, TT, EH])
        einv = sb("einv", [P, TT, EH])
        last_dot = sb("last_dot", [P, TT])
        idx = sb("idx", [P, TT, SEL], U32)
        valid = sb("valid", [P, TT, SEL])
        wlast = sb("wlast", [P, TT, SEL])
        soft = sb("soft", [P, TT, SEL])
        dots = sb("dots", [P, TT, SEL])
        act_in = sb("act_in", [P, TT, SEL])
        act_out = sb("act_out", [P, TT, SEL])
        gall = sb("gall", [P, TT, SEL])
        gvalid = sb("gvalid", [P, TT, SEL])
        glast = sb("glast", [P, TT, SEL])
        invalid = glast
        glsum = sb("glsum", [P, TT])

        S = [ps("S0", [P, 2, 512]), ps("S1", [P, 2, 512])]
        T = ps("T", [P, 2, 512])
        O = ps("O", [P, 512])
        M = ps("M", [P, 512])
        accs = [S[0][:, 0], S[0][:, 1], S[1][:, 0], S[1][:, 1]]
        gu_banks = [(T[:, 0], T[:, 1]), (O[:, :], M[:, :])]
        rot_banks = [O[:, :], M[:, :]]
        v_bank = lambda t: T[:, t] if t < 2 else M[:, :]
        fq_banks = [T[:, 0], T[:, 1], O[:, :], M[:, :]]
        spread_bank = lambda n: M[:, :] if n < 2 * TT - 1 else accs[3]
        EARLY, LATE = slice(0, N - P), slice(N - P, N)
        CROSS_PARTS = slice(P, 3 * P), slice(3 * P, N), slice(0, P)

        const_in, const_ready, rows_clear = sem("const_in"), sem("const_ready"), sem("rows_clear")
        w_in = [sem(f"w_in{i}") for i in range(RING)]
        x_in, xT_in, ctx_in = sem("x_in"), sem("xT_in"), sem("ctx_in")
        row_in = [sem(f"row_in{i}") for i in range(SLOTS)]
        out_done = [sem(f"out_done{i}") for i in range(TT)]
        proj_done, rot_done, s_done, t_done, pv_done = (sem(n) for n in (
            "proj_done", "rot_done", "s_done", "t_done", "pv_done"))
        spread_done, oproj_done, xt_done, kv2_done, q2_done = (sem(n) for n in (
            "spread_done", "oproj_done", "xt_done", "kv2_done", "q2_done"))
        qf_done, sim_done, gu_done, down_done = (sem(n) for n in ("qf_done", "sim_done", "gu_done", "down_done"))
        qk0_ready, v_ready, k2_ready, p_ready = sem("qk0_ready"), sem("v_ready"), sem("k2_ready"), sem("p_ready")
        pt_ready, spread_ready, xt_ready, q2_ready = (sem(n) for n in ("pt_ready", "spread_ready", "xt_ready", "q2_ready"))
        qf_ready, sim_ready, gate_ready = sem("qf_ready"), sem("sim_ready"), sem("gate_ready")
        expo_ready, silu_ready = sem("expo_ready"), sem("silu_ready")
        rot_used, rope_ready, nmax_ready, attn_ready = (sem(n) for n in ("rot_used", "rope_ready", "nmax_ready", "attn_ready"))
        rinv_ready = sem("rinv_ready")
        y_ready, xn_ready, v2_ready, hid_ready = sem("y_ready"), sem("xn_ready"), sem("v2_ready"), sem("hid_ready")
        acc_taken, shifted_ready, idx_ready = sem("acc_taken"), sem("shifted_ready"), sem("idx_ready")
        weights_ready, diag_ready = sem("weights_ready"), sem("diag_ready")
        act_in_ready, rows_used, out_ready = sem("act_in_ready"), sem("rows_used"), sem("out_ready")
        xb_ready, xb2_ready, cosq_ready = sem("xb_ready"), sem("xb2_ready"), sem("cosq_ready")
        dve_chain, pool_gate = sem("dve_chain"), sem("pool_gate")

        block = ctx.enter_context(nc.Block())
        NCONST = 15

        @block.sync
        def _(sp):
            def load(k):
                sp.dma_start(ring[:, k % RING, :], pieces[k]).then_inc(w_in[k % RING], 16)

            sp.dma_start(xT[:, :, :], x_feat[0]).then_inc(xT_in, 16)
            load(W_Q)
            for dst, src in ((identf[:, :], consts[:, 0:128]), (rotate[:, :], consts[:, 128:256]),
                             (cos[:, :], consts[:, 256:768]), (sin[:, :], consts[:, 768:1280]),
                             (vp[:, 0:128], consts[:, 1280:1408]), (vp[:, 128:128 + LKV], consts[:, 1408:1408 + LKV]),
                             (iota8[:, :], consts[:, 1536:1544]),
                             (keysT[:, :, :, :].rearrange("p a m k -> p (a m k)"), keys),
                             (bo_all[:, :], rows[0:1, :].to_broadcast([P, D])),
                             (bo2_all[:, :], rows[1:2, :].to_broadcast([P, D])),
                             (bv2_all[:, :], rows[2:3, :].to_broadcast([P, D])),
                             (last_down[:, :], table[LAST:EXPERTS, 0:D].to_broadcast([P, D])),
                             (last_up[:, :], table[LAST:EXPERTS, D:EROW].to_broadcast([P, D])),
                             (bcols[:, 0, :], cols[:, 0:CC]), (bcols[:, 1, :], cols[:, CC:2 * CC])):
                sp.dma_start(dst, src).then_inc(const_in, 16)

            def batch(b):
                if earlier(b):
                    sp.wait_ge(proj_done, at(b, 12, 0))
                    sp.dma_start(xT[:, :, :], x_feat[b]).then_inc(xT_in, 16)
                if earlier(b):
                    sp.wait_ge(y_ready, at(b, 8, 0))
                sp.dma_start(xres[:, :, :], x_tok[b]).then_inc(x_in, 16)
                if earlier(b):
                    sp.wait_ge(kv2_done, at(b, 2, 0))
                sp.dma_start(ctxT[:, :, :], ctx_feat[b]).then_inc(ctx_in, 16)
                for k in range(RING):
                    if earlier(b) and k % 3 < 2:
                        sp.wait_ge(gu_done, at(b, CHUNKS, 2 * (k // 3) - 2))
                    if earlier(b) and k % 3 == 2:
                        sp.wait_ge(down_done, at(b, CHUNKS, 2 * (k // 3) - 2))
                    if earlier(b) or k > W_Q:
                        load(k)
                for h in range(4):
                    sp.wait_ge(proj_done, at(b, 12, 2 * h + 2))
                    load(W_O + h)
                sp.wait_ge(proj_done, at(b, 12, 12))
                load(W_Q2)
                load(W_Q2 + 1)
                sp.wait_ge(oproj_done, at(b, 8, TT))
                load(W_V2)
                load(W_V2 + 1)
                sp.wait_ge(kv2_done, at(b, 2, 1))
                load(W_O2)
                load(W_O2 + 1)
                for h in range(2):
                    sp.wait_ge(q2_done, at(b, CC, 2 * h + 2))
                    load(W_FQ + h)
                sp.wait_ge(kv2_done, at(b, 2, 2))
                load(W_MLP)
                load(W_MLP + 1)
                sp.wait_ge(oproj_done, at(b, 8, 8))
                load(W_MLP + 2)
                load(W_MLP + 3)
                for h in range(2):
                    sp.wait_ge(qf_done, at(b, CC, 2 * h + 2))
                    load(W_MLP + 4 + h)
                for g in range(2, CHUNKS // 2):
                    sp.wait_ge(gu_done, at(b, CHUNKS, 2 * g - 2))
                    load(W_MLP + 3 * g)
                    load(W_MLP + 3 * g + 1)
                    sp.wait_ge(down_done, at(b, CHUNKS, 2 * g - 2))
                    load(W_MLP + 3 * g + 2)

            batch(0)
            with sp.Fori(1, NB) as b:
                batch(b)
            for t in range(TT):
                sp.wait_ge(out_done[t], 16 * NB)

        @block.tensor
        def _(pe):
            mm = nc.tensor.matmul

            def weights(b, k):
                pe.wait_ge(w_in[k % RING], at(b, 16 * LAPS, 16 * (k // RING + 1)))
                return ring[:, k % RING, :].rearrange("p (c f) -> p c f", c=CC)

            def by_feature(b, dst, piece, j, rhs):
                w = weights(b, piece + j // 2)
                for c in range(CC):
                    last = mm(dst, lhsT=w[:, c, (j % 2) * P:(j % 2 + 1) * P], rhs=rhs[:, c, :],
                              start=(c == 0), stop=(c == CC - 1))
                return last

            def by_token_half(b, dst, piece, lhs, h):
                w = weights(b, piece + h)
                for c in range(CC):
                    last = mm(dst[:, h * 256:(h + 1) * 256], lhsT=lhs[:, c, :], rhs=w[:, c, :],
                              start=(c == 0), stop=(c == CC - 1))
                return last

            def by_token(b, dst, piece, lhs):
                by_token_half(b, dst, piece, lhs, 0)
                return by_token_half(b, dst, piece, lhs, 1)

            def project_qk(b, i):
                if i == 0:
                    pe.wait_ge(xT_in, at(b, 16, 16))
                if i < 2:
                    if earlier(b):
                        pe.wait_ge(hid_ready, at(b, CHUNKS, -1))
                else:
                    pe.wait_ge(qk0_ready, at(b, 8, i - 1))
                by_feature(b, T[:, i % 2], W_Q if i < 4 else W_K, i % 4, xT).then_inc(proj_done, 1)

            def rotate_qk(b, i):
                pe.wait_ge(qk0_ready, at(b, 8, i + 1))
                if i == 0 and not earlier(b):
                    pe.wait_ge(const_ready, 1)
                if i < 2:
                    if earlier(b):
                        pe.wait_ge(hid_ready, at(b, CHUNKS, 0))
                else:
                    pe.wait_ge(rot_used, at(b, 8, i - 1))
                mm(rot_banks[i % 2], lhsT=rotate[:, :], rhs=qk0[:, i % 2, :], start=True, stop=True).then_inc(rot_done, 1)

            def project_v(b, t, h):
                if t < 2 and h == 0:
                    pe.wait_ge(qk0_ready, at(b, 8, 7 + t))
                if t == 2 and h == 0:
                    pe.wait_ge(rot_used, at(b, 8, 8))
                if t == 3 and h == 0:
                    pe.wait_ge(v_ready, at(b, TT, t))
                last = by_token_half(b, v_bank(t), W_V, xT[:, :, t * P:(t + 1) * P], h)
                if h == 1:
                    last.then_inc(proj_done, 1)

            def self_scores(b, u):
                t, p = divmod(u, PAIRS)
                width = (t + 1) * P
                if u == 0:
                    pe.wait_ge(rope_ready, at(b, 8, 8))
                    if earlier(b):
                        pe.wait_ge(acc_taken, at(b, TT, 0))
                if u >= 2:
                    pe.wait_ge(p_ready, at(b, UNITS, u - 1))
                for hh in range(2):
                    r = 64 * (p % 2) + 32 * hh
                    q = qT[r:r + 32, p // 2, t * P:width]
                    if t > 0:
                        mm(S[u % 2][:, hh, 0:t * P], lhsT=q, rhs=kT[r:r + 32, p // 2, 0:t * P], start=True, stop=True)
                    mm(S[u % 2][:, hh, t * P:width], lhsT=q, rhs=kT[r:r + 32, p // 2, t * P:width], start=True, stop=False)
                for hh in range(2):
                    last = mm(S[u % 2][:, hh, t * P:width], lhsT=identh[:, :], rhs=maskh[:, :], start=False, stop=True)
                last.then_inc(s_done, 1)

            def self_turn(b, u):
                t = u // PAIRS
                pe.wait_ge(p_ready, at(b, UNITS, u + 1))
                for hh in range(2):
                    if u == 0:
                        pe.wait_ge(v_ready, at(b, TT, hh + 1))
                    else:
                        pe.wait_ge(pt_ready, at(b, 2 * UNITS, 2 * (u - 1) + hh + 1))
                    for k in range(t + 1):
                        last = nc.tensor.transpose(T[:, hh, k * P:(k + 1) * P], prob[:, u % 2, hh, k * P:(k + 1) * P],
                                                   identf[:, :])
                    last.then_inc(t_done, 1)

            def self_values(b, u):
                t, p = divmod(u, PAIRS)
                if p == 0:
                    pe.wait_ge(v_ready, at(b, TT, t + 1))
                if p == 0 and t > 0:
                    pe.wait_ge(attn_ready, at(b, 8, t))
                pe.wait_ge(pt_ready, at(b, 2 * UNITS, 2 * u + 2))
                for k in range(t + 1):
                    for hh in range(2):
                        h = 2 * p + hh
                        r = 64 * (p % 2) + 32 * hh
                        last = mm(O[r:r + HD, (p // 2) * P:(p // 2 + 1) * P], lhsT=vtok[:, k, h * HD:(h + 1) * HD],
                                  rhs=pT[:, u % 2, hh, k * P:(k + 1) * P], start=(k == 0), stop=(k == t))
                last.then_inc(pv_done, 1)

            def spread_sums(b, n):
                pe.wait_ge(rinv_ready, at(b, 8, n + 1))
                if n == 0:
                    pe.wait_ge(v_ready, at(b, TT, TT))
                if 0 < n <= TT:
                    pe.wait_ge(xt_ready, at(b, 8, n))
                if TT < n < 2 * TT - 1:
                    pe.wait_ge(y_ready, at(b, 8, n))
                dst = spread_bank(n)
                for c in range(CC):
                    last = nc.tensor.transpose(dst[:, c * P:(c + 1) * P], rinvs[:, c * P:(c + 1) * P], identf[:, :])
                last.then_inc(spread_done, 1)

            def project_out(b, n):
                pe.wait_ge(attn_ready, at(b, 8, n + 1))
                if n == 2 * TT - 1:
                    pe.wait_ge(y_ready, at(b, 8, n))
                by_token(b, M[:, :], W_O if n < TT else W_O2, attnT).then_inc(oproj_done, 1)

            def turn_norm(b, n):
                pe.wait_ge(xn_ready, at(b, 8, n + 1))
                src = xres[:, n, :] if n < TT else x2[:, cross_tile(n - TT), :]
                dst = M[:, :] if n < TT else accs[n - TT]
                for c in range(CC):
                    last = nc.tensor.transpose(dst[:, c * P:(c + 1) * P], src[:, c * P:(c + 1) * P], identf[:, :])
                last.then_inc(xt_done, 1)

            def project_k2(b):
                pe.wait_ge(ctx_in, at(b, 16, 16))
                pe.wait_ge(pt_ready, at(b, 2 * UNITS, 2 * SELF_UNITS - 1))
                for j in range(CC):
                    last = by_feature(b, T[:, 0, j * LKV:(j + 1) * LKV], W_K2, j, ctxT)
                last.then_inc(kv2_done, 1)

            def project_v2(b, h):
                if h == 0:
                    pe.wait_ge(pt_ready, at(b, 2 * UNITS, 2 * SELF_UNITS))
                last = by_token_half(b, T[0:LKV, 1], W_V2, ctxT, h)
                if h == 1:
                    last.then_inc(kv2_done, 1)

            def by_feature_split(b, dst, piece, j, rhs, columns):
                w = weights(b, piece + j // 2)
                for c in range(CC):
                    last = mm(dst[:, columns], lhsT=w[:, c, (j % 2) * P:(j % 2 + 1) * P], rhs=rhs[:, c, columns],
                              start=(c == 0), stop=(c == CC - 1))
                return last

            def project_q2_early(b, j):
                if j == 0:
                    pe.wait_ge(xt_ready, at(b, 8, TT - 1))
                if j == 2:
                    pe.wait_ge(p_ready, at(b, UNITS, SELF_UNITS))
                by_feature_split(b, accs[j], W_Q2, j, actT, EARLY)

            def project_q2_late(b, j):
                if j == 0:
                    pe.wait_ge(xt_ready, at(b, 8, TT))
                by_feature_split(b, accs[j], W_Q2, j, actT, LATE).then_inc(q2_done, 1)

            def cross_scores(b, v):
                t, g = cross_tile(v // 2), v % 2
                if v == 0:
                    pe.wait_ge(k2_ready, at(b, 1, 1))
                if v >= 2:
                    pe.wait_ge(p_ready, at(b, UNITS, SELF_UNITS + v - 1))
                for c in range(CC):
                    if v == 0:
                        pe.wait_ge(q2_ready, at(b, CC, max(2, c + 1)))
                    if v == 1 and c == 0:
                        pe.wait_ge(q2_ready, at(b, CC, CC))
                    for hh in range(2):
                        r = 64 * g + 32 * hh
                        last = mm(S[v % 2][:, hh, c * LKV:(c + 1) * LKV], lhsT=qT[r:r + 32, c, t * P:(t + 1) * P],
                                  rhs=k2T[r:r + 32, c, :], start=True, stop=(t > 0))
                        if t == 0:
                            last = mm(S[v % 2][:, hh, c * LKV:(c + 1) * LKV], lhsT=identb[:, :], rhs=maskb[:, :],
                                      start=False, stop=True)
                last.then_inc(s_done, 1)

            def cross_turn(b, v):
                u = SELF_UNITS + v
                pe.wait_ge(p_ready, at(b, UNITS, u + 1))
                for hh in range(2):
                    if v == 0:
                        pe.wait_ge(k2_ready if hh == 0 else v2_ready, at(b, 1, 1))
                    else:
                        pe.wait_ge(pt_ready, at(b, 2 * UNITS, 2 * (u - 1) + hh + 1))
                    for c in range(CC):
                        last = nc.tensor.transpose(T[0:LKV, hh, c * P:(c + 1) * P],
                                                   prob[:, v % 2, hh, c * LKV:(c + 1) * LKV], identf[:, :])
                    last.then_inc(t_done, 1)

            def cross_values(b, v):
                g = v % 2
                u = SELF_UNITS + v
                if g == 0:
                    pe.wait_ge(attn_ready, at(b, 8, TT + v // 2))
                for hh in range(2):
                    pe.wait_ge(pt_ready, at(b, 2 * UNITS, 2 * u + hh + 1))
                    r = 64 * g + 32 * hh
                    for c in range(CC):
                        h = 4 * c + 2 * g + hh
                        last = mm(O[r:r + HD, c * P:(c + 1) * P], lhsT=v2[0:LKV, h * HD:(h + 1) * HD],
                                  rhs=pT[0:LKV, v % 2, hh, c * P:(c + 1) * P], start=True, stop=True)
                last.then_inc(pv_done, 1)

            def project_fq(b, j, part):
                if j == 0:
                    pe.wait_ge(xt_ready, at(b, 8, 6 + part))
                if j == 3 and part == 0:
                    pe.wait_ge(y_ready, at(b, 8, 8))
                last = by_feature_split(b, fq_banks[j], W_FQ, j, actT, CROSS_PARTS[part])
                if part == 2:
                    last.then_inc(qf_done, 1)

            def similarities(b, t):
                if t >= 2:
                    pe.wait_ge(sim_ready, at(b, TT, t - 1))
                for m in range(4):
                    if t == 0:
                        pe.wait_ge(qf_ready, at(b, CC, m + 1))
                    for j in range(2):
                        last = mm(S[t % 2][:, j, m * KEYS:(m + 1) * KEYS], lhsT=kT[64 * j:64 * j + 64, m, t * P:(t + 1) * P],
                                  rhs=keysT[64 * j:64 * j + 64, m // 2, m % 2, :], start=True, stop=True)
                last.then_inc(sim_done, 1)

            def gate_up(b, k):
                if k >= 2:
                    pe.wait_ge(hid_ready, at(b, CHUNKS, k - 1))
                for side in range(2):
                    w = weights(b, W_MLP + 3 * (k // 2) + side)
                    for c in range(CC):
                        last = mm(gu_banks[k % 2][side], lhsT=w[:, c, (k % 2) * P:(k % 2 + 1) * P], rhs=actT[:, c, :],
                                  start=(c == 0), stop=(c == CC - 1))
                last.then_inc(gu_done, 1)

            def down(b, k):
                weights(b, W_MLP + 3 * (k // 2) + 2)
                w = ring[:, (W_MLP + 3 * (k // 2) + 2) % RING, (k % 2) * D:(k % 2 + 1) * D]
                pe.wait_ge(hid_ready, at(b, CHUNKS, k + 1))
                if k == 0:
                    pe.wait_ge(sim_ready, at(b, TT, TT))
                for t in range(TT):
                    last = mm(accs[t], lhsT=hid[k % 2][:, t * P:(t + 1) * P], rhs=w,
                              start=(k == 0), stop=(k == CHUNKS - 1))
                last.then_inc(down_done, 1)

            def batch(b):
                for i in range(8):
                    project_qk(b, i)
                    if i == 1 and earlier(b):
                        down(b - 1, CHUNKS - 1)
                    if i >= 1:
                        rotate_qk(b, i - 1)
                for h in range(2):
                    project_v(b, 0, h)
                rotate_qk(b, 7)
                for h in range(2):
                    project_v(b, 1, h)
                for u in range(SELF_END):
                    tile, stage = divmod(u - PAIRS, PAIRS)
                    if u < SELF_UNITS:
                        self_scores(b, u)
                    if u in (1, 2):
                        project_v(b, 2, u - 1)
                    if u in (4, 5):
                        project_v(b, 3, u - 4)
                    if u == SELF_UNITS:
                        self_values(b, u - 2)
                    if 1 <= u <= SELF_UNITS:
                        self_turn(b, u - 1)
                    if stage == 1 and tile >= 0:
                        spread_sums(b, tile)
                    if 2 <= u <= SELF_UNITS + 1 and u != SELF_UNITS:
                        self_values(b, u - 2)
                    if u == SELF_UNITS + 2:
                        project_k2(b)
                    if stage == 3 and tile >= 0:
                        project_out(b, tile)
                    if stage == 6 and tile >= 0:
                        turn_norm(b, tile)
                for j in range(CC):
                    project_q2_early(b, j)
                turn_norm(b, TT - 1)
                project_v2(b, 0)
                for j in range(CC):
                    project_q2_late(b, j)
                for v in range(CROSS_UNITS + 3):
                    if v < CROSS_UNITS:
                        cross_scores(b, v)
                    if v == 1:
                        project_v2(b, 1)
                    if v == CROSS_UNITS:
                        turn_norm(b, TT)
                        cross_values(b, v - 2)
                    if 1 <= v <= CROSS_UNITS:
                        cross_turn(b, v - 1)
                    if v >= 3 and v % 2 == 1:
                        spread_sums(b, TT + v // 2 - 1)
                    if v == 2 * TT + 1:
                        turn_norm(b, TT + 1)
                    if 2 <= v <= CROSS_UNITS + 1 and v != CROSS_UNITS:
                        cross_values(b, v - 2)
                    if v == 2 * TT + 2:
                        project_fq(b, 0, 0)
                    if v >= 4 and v % 2 == 0:
                        project_out(b, TT + v // 2 - 2)
                project_fq(b, 1, 0)
                turn_norm(b, TT + 2)
                project_fq(b, 2, 0)
                project_fq(b, 3, 0)
                turn_norm(b, TT + 3)
                for part in (1, 2):
                    for j in range(CC):
                        project_fq(b, j, part)
                for t in range(TT):
                    similarities(b, t)
                for k in range(CHUNKS):
                    gate_up(b, k)
                    if k >= 1:
                        down(b, k - 1)

            batch(0)
            with pe.Fori(1, NB) as b:
                batch(b)
            down(NB - 1, CHUNKS - 1)
            pe.wait_ge(acc_taken, TT * NB)
            for q in range(NOW_UNITS, EUNITS):
                t, h = divmod(q, EH)
                for e in range(TOPK):
                    g = q * TOPK + e
                    pe.wait_ge(row_in[g % SLOTS], at(NB - 1, 16 * (GATHERS // SLOTS), 16 * (g // SLOTS + 1)))
                    pe.wait_ge(diag_ready, (q - NOW_UNITS) * TOPK + e + 1)
                    last = mm(accs[t], lhsT=diags[:, q % 2, e, :], rhs=rowsG[:, g % SLOTS, D:EROW],
                              start=(h == 0 and e == 0), stop=(h == EH - 1 and e == TOPK - 1))
                    if e % 2 == 1:
                        last.then_inc(rows_used, 1)

        @block.scalar
        def _(act):
            def copy(dst, src, bias=0.0, scale=1.0):
                return nc.scalar.activation(dst, src, ACT.Identity, bias=bias, scale=scale)

            def expert_silu(b, q):
                t, h = divmod(q, EH)
                act.wait_ge(act_in_ready, at(b, EUNITS, q + 1))
                part = slice(h * TOPK, (h + 1) * TOPK)
                if q < NOW_UNITS:
                    nc.scalar.activation(act_out[:, t, part], act_in[:, t, part], ACT.Silu).then_inc(silu_ready, 1)
                else:
                    nc.scalar.activation(act_out[:, t, part], act_in[:, t, part], ACT.Exp, scale=-1.0).then_inc(silu_ready, 1)

            def expert_silus(b, steps):
                for n in steps:
                    if n % STEPS == TOPK - AHEAD:
                        expert_silu(b, n // STEPS)

            def take_turned(b, u, rows_, width):
                for hh in range(2):
                    act.wait_ge(t_done, at(b, 2 * UNITS, 2 * u + hh + 1))
                    if u >= 2:
                        act.wait_ge(pv_done, at(b, UNITS, u - 1))
                    copy(pT[0:rows_, u % 2, hh, 0:width], T[0:rows_, hh, 0:width]).then_inc(pt_ready, 1)

            def self_exp(b, u):
                t, p = divmod(u, PAIRS)
                width = (t + 1) * P
                act.wait_ge(nmax_ready, at(b, UNITS, u + 1))
                for hh in range(2):
                    h = 2 * p + hh
                    last = nc.scalar.activation(prob[:, u % 2, hh, 0:width], S[u % 2][:, hh, 0:width], ACT.Exp,
                                                bias=nmax[:, u % 2, hh:hh + 1], accum_out=rsum[:, t % 2, h:h + 1])
                last.then_inc(p_ready, 1)

            def cross_exp(b, v):
                t, g = divmod(v, 2)
                act.wait_ge(nmax_ready, at(b, UNITS, SELF_UNITS + v + 1))
                for hh in range(2):
                    for c in range(CC):
                        h = 4 * c + 2 * g + hh
                        last = nc.scalar.activation(prob[:, v % 2, hh, c * LKV:(c + 1) * LKV],
                                                    S[v % 2][:, hh, c * LKV:(c + 1) * LKV], ACT.Exp,
                                                    bias=nmax[:, v % 2, hh * CC + c:hh * CC + c + 1],
                                                    accum_out=rsum[:, t % 2, h:h + 1])
                last.then_inc(p_ready, 1)

            def take_v(b, t):
                act.wait_ge(proj_done, at(b, 12, 9 + t))
                copy(vtok[:, t, :], v_bank(t)).then_inc(v_ready, 1)

            def take_spread(b, n):
                act.wait_ge(spread_done, at(b, 8, n + 1))
                copy(rinvs[:, :], spread_bank(n)).then_inc(spread_ready, 1)

            def take_norm(b, n):
                act.wait_ge(xt_done, at(b, 8, n + 1))
                t = n if n < TT else cross_tile(n - TT)
                src = M[:, :] if n < TT else accs[n - TT]
                copy(actT[:, :, t * P:(t + 1) * P], src.rearrange("p (c k) -> p c k", c=CC)).then_inc(xt_ready, 1)

            def batch(b, first):
                for i in range(8):
                    act.wait_ge(proj_done, at(b, 12, i + 1))
                    if i >= 2:
                        act.wait_ge(rot_done, at(b, 8, i - 1))
                        act.wait_ge(cosq_ready, at(b, 8, i - 1))
                    copy(qk0[:, i % 2, :], T[:, i % 2], scale=SELF_SCALE if i < 4 else 1.0).then_inc(qk0_ready, 1)
                    if not first and i >= 1:
                        expert_silus(b - 1, deferred_steps(i - 1))
                take_v(b, 0)
                if not first:
                    for place in (BESIDE_V - 2, BESIDE_V - 1, BESIDE_V):
                        expert_silus(b - 1, deferred_steps(place))
                take_v(b, 1)
                for u in range(SELF_END):
                    if 1 <= u <= SELF_UNITS:
                        take_turned(b, u - 1, P, ((u - 1) // PAIRS + 1) * P)
                    if u < SELF_UNITS:
                        self_exp(b, u)
                    if u in (2, 5):
                        take_v(b, 2 + u // 5)
                    tile, stage = divmod(u - PAIRS, PAIRS)
                    if stage == 1 and tile >= 0:
                        take_spread(b, tile)
                    if u < SELF_UNITS and not first:
                        expert_silus(b - 1, deferred_steps(FIRST_SELF + u))
                    if u == SELF_UNITS + 2:
                        act.wait_ge(kv2_done, at(b, 2, 1))
                        for j in range(CC):
                            last = copy(k2T[:, j, :], T[:, 0, j * LKV:(j + 1) * LKV], bias=bcols[:, 1, j:j + 1])
                        last.then_inc(k2_ready, 1)
                        if not first:
                            expert_silus(b - 1, deferred_steps(BESIDE_OUT))
                    if stage == 6 and tile >= 0:
                        take_norm(b, tile)
                if not first:
                    expert_silus(b - 1, deferred_steps(BESIDE_NORM))
                    expert_silus(b - 1, deferred_steps(BESIDE_Q2))
                take_norm(b, TT - 1)
                for j in range(CC):
                    act.wait_ge(q2_done, at(b, CC, j + 1))
                    copy(qT[:, j, :], accs[j], bias=bq_scaled[:, j:j + 1], scale=CROSS_SCALE).then_inc(q2_ready, 1)
                for v in range(CROSS_UNITS + 2):
                    if v < CROSS_UNITS - 1:
                        cross_exp(b, v)
                    if 1 <= v <= CROSS_UNITS:
                        take_turned(b, SELF_UNITS + v - 1, LKV, CC * P)
                    if v >= 3 and v % 2 == 1:
                        take_spread(b, TT + v // 2 - 1)
                    if v == CROSS_UNITS - 1:
                        cross_exp(b, v)
                    if v >= CROSS_UNITS:
                        take_norm(b, TT + v - CROSS_UNITS)
                    if v < CROSS_UNITS and not first:
                        expert_silus(b - 1, deferred_steps(FIRST_CROSS + v))
                for t in range(2, TT):
                    take_norm(b, TT + t)
                for j in range(CC):
                    act.wait_ge(qf_done, at(b, CC, j + 1))
                    copy(kT[:, j, :], fq_banks[j]).then_inc(qf_ready, 1)
                for t in range(TT):
                    act.wait_ge(sim_done, at(b, TT, t + 1))
                    copy(vp[:, t * 1024:(t + 1) * 1024].rearrange("p (j k) -> p j k", j=2), S[t % 2][:, :, :]).then_inc(sim_ready, 1)
                for k in range(CHUNKS):
                    act.wait_ge(gu_done, at(b, CHUNKS, k + 1))
                    if k >= 2:
                        act.wait_ge(hid_ready, at(b, CHUNKS, k - 1))
                    nc.scalar.activation(gate[k % 2], gu_banks[k % 2][0], ACT.Silu).then_inc(gate_ready, 1)
                    if k == TT - 1:
                        act.wait_ge(shifted_ready, at(b, TT, TT))
                        nc.scalar.activation(expo[:, :, :, :], expo[:, :, :, :], ACT.Exp).then_inc(expo_ready, 1)
                    if k >= TT:
                        expert_silus(b, mlp_steps(k))

            batch(0, True)
            with act.Fori(1, NB) as b:
                batch(b, False)
            for q in range(NOW_UNITS, EUNITS):
                expert_silu(NB - 1, q)
                if q == NOW_UNITS:
                    act.wait_ge(down_done, CHUNKS * NB)
                if q >= NOW_UNITS + 2:
                    act.wait_ge(rows_used, at(NB - 1, GATHERS // 2, (q - 1) * TOPK // 2))
                act.wait_ge(weights_ready, q - NOW_UNITS + 1)
                for e in range(TOPK):
                    column = q % EH * TOPK + e
                    nc.scalar.activation(diags[:, q % 2, e, :], identf[:, :], ACT.Identity,
                                         scale=gvalid[:, q // EH, column:column + 1]).then_inc(diag_ready, 1)

        @block.vector
        def _(dve):
            count = [0]

            def link(ins):
                mark(ins)
                dve.wait_ge(dve_chain, count[0])

            def mark(ins):
                count[0] += 1
                ins.then_inc(dve_chain, 1)

            def clear_links():
                dve.sem_clear(dve_chain)
                count[0] = 0

            v = nc.vector
            bc = lambda ap, axis, shape: ap.unsqueeze(axis).to_broadcast(shape)

            def rope(b, i):
                dve.wait_ge(rot_done, at(b, 8, i + 1))
                v.tensor_tensor(rot[i % 2], rot_banks[i % 2], sin[:, :], ALU.mult).then_inc(rot_used, 1)
                dst = (qT if i < 4 else kT)[:, i % 4, :]
                dve.wait_ge(cosq_ready, at(b, 8, i + 1))
                dve.wait_ge(rot_used, at(b, 8, i + 1))
                v.tensor_tensor(dst, dst, rot[i % 2], ALU.add).then_inc(rope_ready, 1)

            def self_max(b, u):
                width = (u // PAIRS + 1) * P
                dve.wait_ge(s_done, at(b, UNITS, u + 1))
                v.tensor_reduce(out=nmax[:, u % 2, 0:2], in_=S[u % 2][:, :, 0:width], axis=AX.X, op=ALU.max,
                                negate=True).then_inc(nmax_ready, 1)

            def cross_max(b, w):
                dve.wait_ge(s_done, at(b, UNITS, SELF_UNITS + w + 1))
                v.tensor_reduce(out=nmax[:, w % 2, 0:8].rearrange("p (h c) -> p h c", h=2),
                                in_=S[w % 2][:, :, 0:CC * LKV].rearrange("p h (c k) -> p h c k", c=CC), axis=AX.X,
                                op=ALU.max, negate=True).then_inc(nmax_ready, 1)

            def invert_sums(b, n):
                dve.wait_ge(p_ready, at(b, UNITS, PAIRS * (n + 1) if n < TT else SELF_UNITS + 2 * (n - TT + 1)))
                link(v.reciprocal(rinv[:, :], rsum[:, n % 2, :]))
                v.tensor_copy(rinvs[:, :].rearrange("p (h d) -> p h d", h=H),
                              bc(rinv[:, :], 2, [P, H, HD])).then_inc(rinv_ready, 1)

            def divide(b, n):
                dve.wait_ge(pv_done, at(b, UNITS, PAIRS * (n + 1) if n < TT else SELF_UNITS + 2 * (n - TT + 1)))
                dve.wait_ge(spread_ready, at(b, 8, n + 1))
                v.tensor_tensor(attnT[:, :, :].rearrange("p c k -> p (c k)"), O[:, :], rinvs[:, :],
                                ALU.mult).then_inc(attn_ready, 1)

            def norm_stats(src, slot):
                link(v.bn_stats(out=stats[:, :], in_=src))
                link(v.bn_aggr(out=mv[:, slot, :], in_=stats[:, :]))

            def norm_scale(n):
                mark(v.tensor_scalar(vhalf[:, 0:n], mv[:, 0:n, 1], -0.5, -0.5 * EPS, ALU.mult, ALU.add))
                link(v.tensor_scalar(veps[:, 0:n], mv[:, 0:n, 1], EPS, None, ALU.add))
                link(v.tensor_scalar(rstd[:, 0:n].bitcast(I32), veps[:, 0:n].bitcast(I32), -0.5, float(0x5F3759DF),
                                     ALU.mult, ALU.add))
                for _ in range(3):
                    if n == 1:
                        link(v.scalar_tensor_tensor(out=rtmp[:, 0:1], in0=rstd[:, 0:1], scalar=vhalf[:, 0:1],
                                                    in1=rstd[:, 0:1], op0=ALU.mult, op1=ALU.mult))
                    else:
                        link(v.tensor_tensor(rtmp[:, 0:n], rstd[:, 0:n], vhalf[:, 0:n], ALU.mult))
                        link(v.tensor_tensor(rtmp[:, 0:n], rtmp[:, 0:n], rstd[:, 0:n], ALU.mult))
                    link(v.scalar_tensor_tensor(out=rstd[:, 0:n], in0=rtmp[:, 0:n], scalar=1.5, in1=rstd[:, 0:n],
                                                op0=ALU.add, op1=ALU.mult))

            def norm_apply(src, dst, slot):
                return v.tensor_scalar(dst, src, mv[:, slot, 0:1], rstd[:, slot:slot + 1], ALU.subtract, ALU.mult)

            def residual_sum(b, n):
                t = n if n < TT else cross_tile(n - TT)
                dst = xres[:, t, :] if n < TT else x2[:, t, :]
                dve.wait_ge(xb_ready if n < TT else xb2_ready, at(b, TT, t + 1))
                dve.wait_ge(oproj_done, at(b, 8, n + 1))
                v.tensor_tensor(dst, M[:, :], xres[:, t, :], ALU.add).then_inc(y_ready, 1)

            def residual_stats(b, n):
                dve.wait_ge(y_ready, at(b, 8, n + 1))
                norm_stats(xres[:, n, :] if n < TT else x2[:, cross_tile(n - TT), :], 0)

            def residual_norm(b, n):
                dst = xres[:, n, :] if n < TT else x2[:, cross_tile(n - TT), :]
                norm_scale(1)
                norm_apply(dst, dst, 0).then_inc(xn_ready, 1)

            def route(b, t):
                dve.wait_ge(sim_ready, at(b, TT, t + 1))
                link(v.tensor_tensor_reduce(out=rinvs[:, :], in0=x2[:, t, :], in1=last_down[:, :],
                                            scale=1.0, scalar=0.0, op0=ALU.mult, op1=ALU.add,
                                            accum_out=last_dot[:, t:t + 1]))
                for half in range(2):
                    for h in range(EH):
                        keysim = sims[:, t, h % 2, 2 * half + h // 2, :]
                        link(v.max(out=top1[:, half, h, :], in_=keysim))
                        place = (half * EH + h) * TOPK
                        last = v.max_index(out=top1i[:, place:place + TOPK], in_max=top1[:, half, h, :], in_values=keysim)
                        if half * EH + h == 2 * EH - 1:
                            link(last)
                link(v.tensor_copy(top1f[:, :, :].rearrange("p a k -> p (a k)"), top1i[:, :]))
                link(v.tensor_tensor(sums[:, :, :, :], bc(top1[:, 0], 3, [P, EH, TOPK, TOPK]),
                                     bc(top1[:, 1], 2, [P, EH, TOPK, TOPK]), ALU.add))
                for h in range(EH):
                    flat = sums[:, h].rearrange("p a c -> p (a c)")
                    link(v.max(out=best[:, h, :], in_=flat))
                    last = v.max_index(out=besti[:, h * TOPK:(h + 1) * TOPK], in_max=best[:, h, :], in_values=flat)
                link(last)
                v.tensor_tensor(expo[:, t, :, :], best[:, :, :], best[:, :, 0:1].to_broadcast([P, EH, TOPK]),
                                ALU.subtract).then_inc(shifted_ready, 1)
                v.tensor_scalar(parts[:, 0, :], besti[:, :], 3, None, ALU.logical_shift_right)
                link(v.tensor_scalar(parts[:, 1, :], besti[:, :], 7, None, ALU.bitwise_and))
                link(v.tensor_copy(partf[:, :], parts[:, :, :].rearrange("p a k -> p (a k)")))
                link(v.tensor_tensor(onehot[:, :, :], bc(partf[:, :], 2, [P, 2 * SEL, TOPK]),
                                     bc(iota8[:, :], 1, [P, 2 * SEL, TOPK]), ALU.is_equal))
                spread = onehot[:, :, :].rearrange("p (a k) c -> p a k c", k=TOPK)
                link(v.tensor_tensor(spread, spread, bc(top1f[:, :, :], 2, [P, 2 * EH, TOPK, TOPK]), ALU.mult))
                link(v.tensor_reduce(out=picked[:, :, :].rearrange("p a k -> p (a k)"), in_=onehot[:, :, :], axis=AX.X,
                                     op=ALU.add))
                link(v.scalar_tensor_tensor(out=idxf[:, t, :], in0=picked[:, 0, :], scalar=float(KEYS), in1=picked[:, 1, :],
                                            op0=ALU.mult, op1=ALU.add))
                v.tensor_copy(idx[:, t, :], idxf[:, t, :]).then_inc(idx_ready, 1)

            def route_weights(b):
                mark(v.tensor_scalar(invalid[:, :, :], idxf[:, :, :], float(LAST), None, ALU.is_ge))
                link(v.tensor_scalar(valid[:, :, :], idxf[:, :, :], float(LAST), None, ALU.is_lt))
                mark(v.tensor_tensor(wlast[:, :, :], invalid[:, :, :], bc(last_dot[:, :], 2, [P, TT, SEL]), ALU.mult))
                dve.wait_ge(expo_ready, at(b, 1, 1))
                flat = expo[:, :, :, :].rearrange("p t h k -> p (t h) k")
                link(v.tensor_reduce(out=esum[:, :, :].rearrange("p t h -> p (t h)"), in_=flat, axis=AX.X, op=ALU.add))
                link(v.reciprocal(einv[:, :, :], esum[:, :, :]))
                link(v.tensor_tensor(soft[:, :, :].rearrange("p t (h k) -> p (t h) k", k=TOPK), flat,
                                     bc(einv[:, :, :].rearrange("p t h -> p (t h)"), 2, [P, TT * EH, TOPK]), ALU.mult))

            def dot(b, q, e):
                t = q // EH
                g = q * TOPK + e
                e += q % EH * TOPK
                dve.wait_ge(row_in[g % SLOTS], at(b, 16 * (GATHERS // SLOTS), 16 * (g // SLOTS + 1)))
                return v.tensor_tensor_reduce(out=rowsG[:, g % SLOTS, 0:D], in0=rowsG[:, g % SLOTS, 0:D],
                                              in1=x2[:, t, :], scale=1.0, scalar=0.0, op0=ALU.mult, op1=ALU.add,
                                              accum_out=dots[:, t, e:e + 1])

            def expert_step(b, n, sums_here=True):
                q, s = divmod(n, STEPS)
                t, h = divmod(q, EH)
                part = slice(h * TOPK, (h + 1) * TOPK)
                if s < TOPK - AHEAD:
                    ins = dot(b, q, s + AHEAD)
                    if s == TOPK - AHEAD - 1:
                        link(ins)
                elif s == TOPK - AHEAD:
                    link(v.tensor_tensor(act_in[:, t, part], dots[:, t, part], valid[:, t, part], ALU.mult))
                    v.tensor_tensor(act_in[:, t, part], act_in[:, t, part], wlast[:, t, part],
                                    ALU.add).then_inc(act_in_ready, 1)
                elif s <= TOPK:
                    if q + 1 < EUNITS:
                        dot(b, q + 1, s - TOPK + AHEAD - 1)
                elif s == TOPK + 1:
                    dve.wait_ge(silu_ready, at(b, EUNITS, q + 1))
                    if q < NOW_UNITS:
                        link(v.tensor_tensor(gall[:, t, part], act_out[:, t, part], soft[:, t, part], ALU.mult))
                    else:
                        mark(v.tensor_tensor(gall[:, t, part], act_in[:, t, part], soft[:, t, part], ALU.mult))
                        link(v.tensor_scalar(act_out[:, t, part], act_out[:, t, part], 1.0, None, ALU.add))
                        link(v.reciprocal(act_out[:, t, part], act_out[:, t, part]))
                        link(v.tensor_tensor(gall[:, t, part], gall[:, t, part], act_out[:, t, part], ALU.mult))
                    ins = v.tensor_tensor(gvalid[:, t, part], gall[:, t, part], valid[:, t, part], ALU.mult)
                    if sums_here:
                        link(ins)
                    else:
                        ins.then_inc(weights_ready, 1)
                        dve.wait_ge(weights_ready, q - NOW_UNITS + 1)
                    mark(v.tensor_tensor(glast[:, t, part], gall[:, t, part], gvalid[:, t, part], ALU.subtract))
                elif sums_here:
                    e = s - TOPK - 2
                    g = q * TOPK + e
                    e += h * TOPK
                    base = y3[:, t, :]
                    if e == 0 and q < NOW_UNITS:
                        base = x2[:, t, :]
                        if earlier(b):
                            dve.wait_ge(out_done[t], at(b, 16, 0))
                    if e % 2 == 0 and e > 0:
                        dve.wait_ge(rows_used, at(b, GATHERS // 2, g // 2))
                    ins = v.scalar_tensor_tensor(out=y3[:, t, :], in0=rowsG[:, g % SLOTS, D:EROW],
                                                 scalar=gvalid[:, t, e:e + 1], in1=base, op0=ALU.mult, op1=ALU.add)
                    if e % 2 == 0:
                        link(ins)
                    else:
                        ins.then_inc(rows_used, 1)

            def finish(b):
                link(v.tensor_reduce(out=glsum[:, :], in_=glast[:, :, :], axis=AX.X, op=ALU.add))
                dve.wait_ge(rows_used, at(b, GATHERS // 2, GATHERS // 2))
                for t in range(TT):
                    link(v.scalar_tensor_tensor(out=y3[:, t, :], in0=last_up[:, :], scalar=glsum[:, t:t + 1],
                                                in1=y3[:, t, :], op0=ALU.mult, op1=ALU.add))
                    norm_stats(y3[:, t, :], t)
                norm_scale(TT)
                for t in range(TT):
                    norm_apply(y3[:, t, :], y3[:, t, :], t).then_inc(out_ready, 1)

            def deferred(b, place):
                for n in deferred_steps(place):
                    expert_step(b - 1, n)

            def add_mlp(b):
                dve.wait_ge(down_done, at(b, CHUNKS, CHUNKS))
                dve.wait_ge(rows_used, at(b, GATHERS // 2, NOW // 2))
                for t in range(TT):
                    begun = t * EH < NOW_UNITS
                    if not begun and earlier(b):
                        dve.wait_ge(out_done[t], at(b, 16, 0))
                    v.tensor_tensor(y3[:, t, :], y3[:, t, :] if begun else x2[:, t, :], accs[t],
                                    ALU.add).then_inc(acc_taken, 1)
                dve.wait_ge(acc_taken, at(b, TT, TT))

            def hidden(b, k):
                dve.wait_ge(gate_ready, at(b, CHUNKS, k + 1))
                if k >= 2:
                    dve.wait_ge(down_done, at(b, CHUNKS, k - 1))
                v.tensor_tensor(hid[k % 2], gate[k % 2], gu_banks[k % 2][1], ALU.mult).then_inc(hid_ready, 1)

            def batch(b, first):
                if not first:
                    deferred(b, START)
                    add_mlp(b - 1)
                for i in range(ROTATIONS):
                    rope(b, i)
                    if not first:
                        deferred(b, FIRST_ROTATION + i)
                if not first:
                    deferred(b, BESIDE_V)
                for u in range(SELF_END):
                    tile, stage = divmod(u - PAIRS, PAIRS)
                    if stage == 4 and tile >= 0:
                        residual_sum(b, tile)
                    if u < SELF_UNITS:
                        self_max(b, u)
                    if stage == 4 and tile >= 0:
                        residual_stats(b, tile)
                    if stage == 0 and tile >= 0:
                        invert_sums(b, tile)
                    if u < SELF_UNITS and not first and stage == 1:
                        deferred(b, FIRST_SELF + u)
                    if stage == 1 and tile >= 0:
                        divide(b, tile)
                    if stage == 5 and tile >= 0:
                        residual_norm(b, tile)
                    if u < SELF_UNITS and not first and stage != 1:
                        deferred(b, FIRST_SELF + u)
                    if u == SELF_UNITS + 2 and not first:
                        deferred(b, BESIDE_OUT)
                if not first:
                    deferred(b, BESIDE_NORM)
                    deferred(b, BESIDE_Q2)
                for w in range(CROSS_UNITS + 5):
                    if w >= 5 and w % 2 == 1:
                        residual_sum(b, TT + w // 2 - 2)
                    if w < CROSS_UNITS:
                        cross_max(b, w)
                    if w == 1:
                        dve.wait_ge(kv2_done, at(b, 2, 2))
                        v.tensor_tensor(v2[0:LKV, :], T[0:LKV, 1], bv2_all[0:LKV, :], ALU.add).then_inc(v2_ready, 1)
                    if w >= 2 and w % 2 == 0 and w // 2 - 1 < TT:
                        invert_sums(b, TT + w // 2 - 1)
                    if w < CROSS_UNITS and w % 2 == 1 and not first:
                        deferred(b, FIRST_CROSS + w)
                    if w >= 3 and w % 2 == 1 and w // 2 - 1 < TT:
                        divide(b, TT + w // 2 - 1)
                    if w >= 5 and w % 2 == 1:
                        residual_stats(b, TT + w // 2 - 2)
                    if w >= 6 and w % 2 == 0:
                        residual_norm(b, TT + w // 2 - 3)
                    if w < CROSS_UNITS and w % 2 == 0 and not first:
                        deferred(b, FIRST_CROSS + w)
                if not first:
                    finish(b - 1)
                for k in range(CHUNKS):
                    if k < TT:
                        route(b, k)
                    if k == TT:
                        for e in range(AHEAD):
                            dot(b, 0, e)
                        route_weights(b)
                    if k >= TT:
                        for n in mlp_steps(k):
                            expert_step(b, n)
                    hidden(b, k)
                clear_links()
            dve.wait_ge(const_in, 16 * NCONST)
            link(v.tensor_copy(identh[:, :], identf[:, :]))
            link(v.tensor_copy(maskh[:, :], vp[:, 0:128]))
            link(v.tensor_scalar(identb[:, :], identf[:, :], HUGE, None, ALU.mult))
            link(v.tensor_copy(maskb[:, :], vp[:, 128:128 + LKV]))
            v.tensor_scalar(bq_scaled[:, :], bcols[:, 0, :], CROSS_SCALE, None, ALU.mult).then_inc(const_ready, 1)
            clear_links()
            batch(0, True)
            with dve.Fori(1, NB) as b:
                batch(b, False)
            deferred(NB, START)
            add_mlp(NB - 1)
            for n in range(NOW_STEPS + PLACES[START], EUNITS * STEPS):
                expert_step(NB - 1, n, sums_here=False)
            for t in range(NOW_UNITS // EH, TT):
                dve.wait_ge(rows_used, at(NB - 1, GATHERS // 2, (t + 1) * SEL // 2))
                link(v.tensor_tensor(y3[:, t, :], y3[:, t, :], accs[t], ALU.add))
            finish(NB - 1)

        @block.gpsimd
        def _(pool):
            g = nc.gpsimd

            def gather(b, n):
                t, e = divmod(n, SEL)
                if n % 2 == 0:
                    if n >= SLOTS or earlier(b):
                        pool.wait_ge(rows_used, at(b, GATHERS // 2, (n - SLOTS) // 2 + 1))
                    if e == 0:
                        pool.wait_ge(idx_ready, at(b, TT, t + 1))
                    pool.sem_inc(pool_gate, 1)
                g.indirect_dma_start(out=rowsG[:, n % SLOTS, :], out_offset=None, in_=table,
                                     in_offset=bass.IndirectOffsetOnAxis(ap=idx[:, t, e:e + 1], axis=0),
                                     bounds_check=LAST - 1, oob_is_err=False).then_inc(row_in[n % SLOTS], 16)

            def store(b, t):
                pool.wait_ge(out_ready, at(b, TT, t + 1))
                pool.sem_inc(pool_gate, 1)
                pool.dma_start(out[b, t], y3[:, t, :]).then_inc(out_done[t], 16)

            def deferred(b, place):
                for n in deferred_rows(place):
                    gather(b - 1, n)

            def batch(b, first):
                pool.wait_ge(x_in, at(b, 16, 16))
                for t in range(TT):
                    g.tensor_tensor(xres[:, t, :], xres[:, t, :], bo_all[:, :], ALU.add).then_inc(xb_ready, 1)
                for i in range(ROTATIONS):
                    pool.wait_ge(qk0_ready, at(b, 8, i + 1))
                    if earlier(b) and i == 1:
                        pool.wait_ge(hid_ready, at(b, CHUNKS, 0))
                    if earlier(b) and i == 3:
                        pool.wait_ge(down_done, at(b, CHUNKS, 0))
                    g.tensor_tensor((qT if i < 4 else kT)[:, i % 4, :], qk0[:, i % 2, :], cos[:, :],
                                    ALU.mult).then_inc(cosq_ready, 1)
                    if not first:
                        deferred(b, i)
                if not first:
                    for place in range(BESIDE_V - 1, FIRST_CROSS):
                        deferred(b, place)
                for t in range(TT):
                    pool.wait_ge(xt_done, at(b, 8, t + 1))
                    g.tensor_tensor(xres[:, t, :], xres[:, t, :], bo2_all[:, :], ALU.add).then_inc(xb2_ready, 1)
                if not first:
                    for place in range(FIRST_CROSS, len(PLACES)):
                        deferred(b, place)
                    for t in range(TT):
                        store(b - 1, t)
                for n in range(NOW + SLOTS):
                    gather(b, n)

            g.memset(rowsG[:, :, :], 0.0).then_inc(rows_clear, 1)
            pool.wait_ge(rows_clear, 1)
            pool.wait_ge(const_in, 16 * NCONST)
            batch(0, True)
            with pool.Fori(1, NB) as b:
                batch(b, False)
            for place in range(len(PLACES)):
                deferred(NB, place)
            for t in range(TT):
                store(NB - 1, t)


def _pieces(w):
    wt = w.T.reshape(CC, P, -1)
    n = wt.shape[2] // 256
    return wt.reshape(CC, P, n, 256).transpose(2, 1, 0, 3).reshape(n, P, PIECE)


def _constants():
    c = np.zeros((P, 1544), np.float32)
    i = np.arange(P)
    c[i, i] = 1.0
    even = i[::2]
    c[even + 1, P + even] = -1.0
    c[even, P + even + 1] = 1.0
    inv_freq = (np.float32(1.0) / np.float32(10000.0) ** (np.arange(0, HD, 2, dtype=np.float32) / np.float32(HD)))
    ang = np.arange(N, dtype=np.float32)[None, :] * inv_freq.astype(np.float32)[(i % HD) // 2][:, None]
    c[:, 256:768] = np.cos(ang)
    c[:, 768:1280] = np.sin(ang)
    c[:, 1280:1408] = np.where(i[None, :] > i[:, None], CAUSAL_ADD, 0.0)
    c[:, 1408:1408 + LKV] = np.where(i[None, :LKV] > i[:, None], -HUGE, 0.0)
    c[:, 1536:1544] = np.arange(TOPK)
    return c


def kernel(**inputs):
    import concourse.bacc as _bacc
    from concourse.bass_utils import run_bass_kernel_spmd as _run

    a = {k: np.asarray(v) for k, v in inputs.items()}
    x, c = a["x"], a["ctx_1024"]
    wg, wu = _pieces(a["L0_ffn_Wg"]), _pieces(a["L0_ffn_Wu"])
    wd = a["L0_ffn_Wd"].T.reshape(CHUNKS // 2, 2, P, D).transpose(0, 2, 1, 3).reshape(CHUNKS // 2, P, PIECE)
    pieces = [_pieces(a[n]) for n in ("L0_attn_Wq", "L0_attn_Wk", "L0_attn_Wv", "L0_attn_Wo", "L0_xattn_Wk",
                                      "L0_xattn_Wq", "L0_xattn_Wv", "L0_xattn_Wo", "L0_ffn_Wq")]
    pieces.append(np.stack([wg, wu, wd], axis=1).reshape(-1, P, PIECE))
    arrays = {
        "x_tok": x.reshape(B, TT, P, D).transpose(0, 2, 1, 3),
        "x_feat": x.transpose(0, 2, 1).reshape(B, CC, P, N).transpose(0, 2, 1, 3),
        "ctx_feat": c.transpose(0, 2, 1).reshape(B, CC, P, LKV).transpose(0, 2, 1, 3),
        "pieces": np.concatenate(pieces),
        "keys": a["L0_ffn_keys"].reshape(2, 2, KEYS, 2, 64).transpose(1, 4, 3, 0, 2).reshape(P, 4 * KEYS),
        "table": np.concatenate([a["L0_ffn_down_embed"], a["L0_ffn_up_embed"]], axis=1),
        "rows": np.stack([a["L0_attn_bo"], a["L0_xattn_bo"], a["L0_xattn_bv"]]),
        "cols": np.concatenate([a["L0_xattn_bq"].reshape(CC, P).T, a["L0_xattn_bk"].reshape(CC, P).T], axis=1),
        "consts": _constants(),
    }
    arrays = {f"{k}_dram": np.ascontiguousarray(v) for k, v in arrays.items()}
    nc = _bacc.Bacc("TRN2", target_bir_lowering=False, num_devices=1)
    args = [nc.dram_tensor(k, v.shape, mybir.dt.from_np(v.dtype), kind="ExternalInput").ap() for k, v in arrays.items()]
    out = nc.dram_tensor("out_dram", (B, TT, P, D), F32, kind="ExternalOutput").ap()
    decoder_layer(nc, *args, out)
    r = _run(nc, [arrays], core_ids=[0])
    return r.results[0]["out_dram"].reshape(B, N, D)
```
